# Optimizing a Trainium2 kernel written in Bass

```python
import numpy as np
import jax
import jax.numpy as jnp

def _softmax(x, axis=-1):
    return jax.nn.softmax(x, axis=axis)

def _gelu(x):
    return jax.nn.gelu(x, approximate=True)

def _silu(x):
    return jax.nn.silu(x)

def _sigmoid(x):
    return jax.nn.sigmoid(x)

def _layernorm(x, axis=-1, eps=1e-05):
    m = jnp.mean(x, axis=axis, keepdims=True)
    v = jnp.var(x, axis=axis, keepdims=True)
    return (x - m) / jnp.sqrt(v + eps)

def _scatter_add(tgt, idx, src, axis=0):
    return tgt.at[idx].add(src)

def _segment_sum(src, seg, n):
    return jax.ops.segment_sum(src, seg, n)
kernel_name = 'mk_macaron_d1_jaxref_r8_e9f776'

def setup_inputs(seed: int=0):
    np.random.seed(seed)
    _w = jnp.asarray

    def _L0_attn_setup():
        import jax, jax.numpy as jnp
        import numpy as np
        DILATION_RATE = 4
        SEGMENT_SIZE = 64
        key = jax.random.key(seed)
        x = jax.random.normal(key, (4, 1024, 128), dtype=jnp.float32)
        return {'x': x}
    _L0_attn_in = _L0_attn_setup()

    def _L0_ffn_setup():
        import jax, jax.numpy as jnp
        import numpy as np
        B, S, D, H, E, K, F = (1, 128, 128, 16, 8, 2, 512)

        def layernorm(x, g, b, eps=1e-05):
            m = x.mean(-1, keepdims=True)
            v = ((x - m) ** 2).mean(-1, keepdims=True)
            return (x - m) * jax.lax.rsqrt(v + eps) * g + b
        key = jax.random.key(seed)
        ks = jax.random.split(key, 8)
        n = lambda k, shape, sc: jax.random.normal(k, shape, dtype=jnp.float32) * sc
        return {'x': n(ks[0], (B, S, D), 1.0), 'w_qkv': n(ks[1], (D, 3 * D), D ** (-0.5)), 'w_o': n(ks[2], (D, D), D ** (-0.5)), 'g1': jnp.ones((D,), jnp.float32), 'b1': jnp.zeros((D,), jnp.float32), 'wg': n(ks[3], (D, E), D ** (-0.5)), 'w1': n(ks[4], (E, D, F), D ** (-0.5)), 'bb1': jnp.zeros((E, F), jnp.float32), 'w2': n(ks[5], (E, F, D), F ** (-0.5)), 'bb2': jnp.zeros((E, D), jnp.float32), 'g2': jnp.ones((D,), jnp.float32), 'b2': jnp.zeros((D,), jnp.float32)}
    _L0_ffn_in = _L0_ffn_setup()
    _d = {'L0_attn_x': _L0_attn_in['x'], 'L0_ffn_w_qkv': _L0_ffn_in['w_qkv'], 'L0_ffn_w_o': _L0_ffn_in['w_o'], 'L0_ffn_g1': _L0_ffn_in['g1'], 'L0_ffn_b1': _L0_ffn_in['b1'], 'L0_ffn_wg': _L0_ffn_in['wg'], 'L0_ffn_w1': _L0_ffn_in['w1'], 'L0_ffn_bb1': _L0_ffn_in['bb1'], 'L0_ffn_w2': _L0_ffn_in['w2'], 'L0_ffn_bb2': _L0_ffn_in['bb2'], 'L0_ffn_g2': _L0_ffn_in['g2'], 'L0_ffn_b2': _L0_ffn_in['b2']}
    _x0 = _d['L0_attn_x']
    _d['L0_attn_x'] = jax.random.normal(jax.random.fold_in(jax.random.key(seed), 1), (16, 256, 128), dtype=_x0.dtype)
    del _x0
    return _d

def reference(L0_attn_x, L0_ffn_w_qkv, L0_ffn_w_o, L0_ffn_g1, L0_ffn_b1, L0_ffn_wg, L0_ffn_w1, L0_ffn_bb1, L0_ffn_w2, L0_ffn_bb2, L0_ffn_g2, L0_ffn_b2):

    def _L0_attn_ref(x):
        import jax, jax.numpy as jnp
        import numpy as np
        DILATION_RATE = 4
        SEGMENT_SIZE = 64
        'LongNet-style dilated attention.\n\n            For each offset in range(dilation_rate): take the strided slice\n            x[:, offset::r, :], split it into segments of length `segment_size`,\n            run full softmax(q k^T / sqrt(d)) v attention inside each segment\n            (q=k=v=the slice; attention dim is the full d_model, matching how the\n            original feeds [B, n_seg, seg, d_model] to FlashAttention), scatter the\n            result back to the strided positions, and average the dilation heads\n            (softmax over uniform logits == 1/r weights).\n\n            Since seq_len % (r * segment_size) == 0, the r strided slices tile the\n            sequence exactly, so we vectorize over offsets with a single reshape:\n            position p = i*r + offset  ->  xr[:, i, offset, :].\n            '
        r, seg = (DILATION_RATE, SEGMENT_SIZE)
        B, S, D = x.shape
        n = S // r
        g = n // seg
        scale = 1.0 / jnp.sqrt(jnp.asarray(D, dtype=x.dtype))
        xs = x.reshape(B, g, seg, r, D)
        scores = jnp.einsum('bgqrd,bgkrd->brgqk', xs, xs) * scale
        probs = jax.nn.softmax(scores, axis=-1)
        out = jnp.einsum('brgqk,bgkrd->bgqrd', probs, xs)
        return out.reshape(B, S, D) / r

    def _L0_ffn_ref(x, w_qkv, w_o, g1, b1, wg, w1, bb1, w2, bb2, g2, b2):
        import jax, jax.numpy as jnp
        import numpy as np
        B, S, D, H, E, K, F = (1, 128, 128, 16, 8, 2, 512)

        def layernorm(x, g, b, eps=1e-05):
            m = x.mean(-1, keepdims=True)
            v = ((x - m) ** 2).mean(-1, keepdims=True)
            return (x - m) * jax.lax.rsqrt(v + eps) * g + b
        b, s, d = x.shape
        hd = d // H
        qkv = x @ w_qkv
        q, k, v = jnp.split(qkv, 3, axis=-1)
        to_heads = lambda t: t.reshape(b, s, H, hd).transpose(0, 2, 1, 3)
        q, k, v = (to_heads(q), to_heads(k), to_heads(v))
        scores = jnp.einsum('bhqd,bhkd->bhqk', q, k) / jnp.sqrt(jnp.float32(hd))
        causal = jnp.tril(jnp.ones((s, s), bool))
        scores = jnp.where(causal, scores, jnp.finfo(scores.dtype).min)
        attn = jax.nn.softmax(scores, axis=-1)
        o = jnp.einsum('bhqk,bhkd->bhqd', attn, v)
        o = o.transpose(0, 2, 1, 3).reshape(b, s, d) @ w_o
        h = layernorm(x + o, g1, b1)
        probs = jax.nn.softmax(h @ wg, axis=-1)
        topv, topi = jax.lax.top_k(probs, K)
        topv = topv / topv.sum(-1, keepdims=True)
        w = (topv[..., None] * jax.nn.one_hot(topi, E, dtype=h.dtype)).sum(-2)
        h1 = jax.nn.gelu(jnp.einsum('bsd,edf->ebsf', h, w1) + bb1[:, None, None, :])
        y = jnp.einsum('ebsf,efd->ebsd', h1, w2) + bb2[:, None, None, :]
        moe = jnp.einsum('ebsd,bse->bsd', y, w)
        return layernorm(h + moe, g2, b2)
    x = L0_attn_x
    x = x + 0.5 * _L0_ffn_ref(_layernorm(x, axis=-1), L0_ffn_w_qkv, L0_ffn_w_o, L0_ffn_g1, L0_ffn_b1, L0_ffn_wg, L0_ffn_w1, L0_ffn_bb1, L0_ffn_w2, L0_ffn_bb2, L0_ffn_g2, L0_ffn_b2)
    x = x + _L0_attn_ref(_layernorm(x, axis=-1))
    x = x + 0.5 * _L0_ffn_ref(_layernorm(x, axis=-1), L0_ffn_w_qkv, L0_ffn_w_o, L0_ffn_g1, L0_ffn_b1, L0_ffn_wg, L0_ffn_w1, L0_ffn_bb1, L0_ffn_w2, L0_ffn_bb2, L0_ffn_g2, L0_ffn_b2)
    return x

_drawn_inputs = setup_inputs


def setup_inputs(seed=0):
    import zlib

    import numpy as np

    out = dict(_drawn_inputs(seed))
    spreads = {'L0_ffn_g1': (1.0, 0.2),
     'L0_ffn_b1': (0.0, 0.1),
     'L0_ffn_bb1': (0.0, 0.303),
     'L0_ffn_bb2': (0.0, 0.1),
     'L0_ffn_g2': (1.0, 0.2),
     'L0_ffn_b2': (0.0, 0.1)}
    factors = {}
    for name, (base, spread) in spreads.items():
        noise = np.random.default_rng([zlib.crc32(name.encode()), seed]).standard_normal(out[name].shape)
        drawn = base * np.exp(spread * noise) if base else spread * noise
        out[name] = jnp.asarray(drawn.astype(out[name].dtype))
    for name, factor in factors.items():
        out[name] = (out[name] * factor).astype(out[name].dtype)
    return out
```

```python
from contextlib import ExitStack

import concourse.bass as bass
from concourse import mybir

ALU = mybir.AluOpType
ACT = mybir.ActivationFunctionType
AX = mybir.AxisListType
F32 = mybir.dt.float32
F32R = mybir.dt.float32r
BF16 = mybir.dt.bfloat16
U32 = mybir.dt.uint32

P = 128
SEQS, S, D = 16, 256, 128
HEADS, HD = 16, 8
E, F = 8, 512
RATE = 4
CHUNKS = SEQS // 2
TOK = 2 * S
TT = TOK // P
FC = F // P
HID = E * FC
GROUPS = 4
EPS = 1e-5
MASKED = -1e30
SLOT = 32

RING = 4
LAG = 3
VLAG = 3
TICKS = HID + LAG

FRONT = {
    0: [("long_stats",)],
    2: [("long_norm",), ("long_turn", 0), ("long_turn", 1)],
    3: [("long_scores", 0), ("long_scores", 1)],
    5: [("long_values", 0), ("long_values", 1)],
    6: [("stats",)],
    8: [("norm",), ("turn", 0), ("turn", 1)],
    9: [("queries_keys", 1), ("queries_keys", 0), ("project_values",), ("spread",)],
    15: [("scores", 0, 0)], 16: [("scores", 0, 1)],
    17: [("scores", 0, 2), ("scores", 0, 3)], 18: [("scores", 1, 0), ("scores", 1, 1)],
    19: [("shift", 0), ("scores", 1, 2), ("scores", 1, 3)],
    20: [("shift", 1)],
    21: [("head", k) for k in range(8)],
    23: [("head", k) for k in range(8, 16)],
    25: [("head", k) for k in range(16, 24)],
    26: [("rows", 0, 0), ("rows", 0, 1)],
    27: [("head", k) for k in range(24, 32)],
    28: [("rows", 1, 0), ("rows", 1, 1)],
    29: [("merge",), ("attn_out",), ("hidden_stats",)],
    30: [("hidden_norm",), ("hidden",), ("split_hidden",)],
    31: [("route",)],
    33: [("gate",), ("gate_turn",)],
}
LONG = {"long_stats", "long_norm", "long_turn", "long_scores", "long_values"}


def front_pieces(kind, tick=None):
    ticks = range(TICKS) if tick is None else [tick]
    return [p for t in ticks for p in FRONT.get(t, []) if kind == "B" or p[0] not in LONG]


def ring_uses(kind):
    uses = []
    for p in front_pieces(kind):
        if p[0] == "scores":
            uses += [p + (part,) for part in range(3)]
        elif p[0] in ("long_turn", "long_scores", "turn", "queries_keys", "project_values", "shift",
                      "head", "rows", "merge", "attn_out", "hidden", "route", "gate_turn"):
            uses.append(p)
    return {use: n for n, use in enumerate(uses)}


RING_USES = {"A": ring_uses("A"), "B": ring_uses("B")}
assert all(len(u) % RING == 0 for u in RING_USES.values())
NORMS = {"A": ["norm", "hidden"], "B": ["long", "norm", "hidden"]}


class LoopCount:

    def __init__(self, eng, c, few, begun):
        self.eng, self.c, self.few, self.begun = eng, c, few, begun
        self.multiples = {}
        self.sum = eng.alloc_register("count")

    def wait_ge(self, handle, factor, more, apart):
        if self.few and more:
            self.eng.reg_mul(self.sum, self.c, factor)
            self.eng.reg_add(self.sum, self.sum, more)
        elif self.few:
            self.eng.reg_mul(self.sum, self.c, factor - 1)
            self.eng.reg_add(self.sum, self.sum, self.c)
        else:
            if factor not in self.multiples:
                self.multiples[factor] = self.eng.alloc_register(f"count_by_{factor}")
                self.eng.reg_mul(self.multiples[factor], self.c, factor)
            if more:
                self.eng.reg_add(self.sum, self.multiples[factor], more)
            else:
                self.eng.reg_mul(self.sum, self.c, factor)
        if apart:
            self.eng.wait_ge(self.begun, 1)
        self.eng.wait_ge(handle, self.sum)


class Job:

    def __init__(self, kind, chunk, a, b, parity, before=None, loop=None):
        self.kind, self.chunk, self.a, self.b, self.parity = kind, chunk, a, b, parity
        self.before = before
        self.loop = loop


def job_at(n):
    order = [("A", 0), ("A", 1)]
    for c in range(CHUNKS - 2):
        order += [("B", c), ("A", c + 2)]
    order += [("B", CHUNKS - 2), ("B", CHUNKS - 1)]
    if not 0 <= n < len(order):
        return None
    kind, chunk = order[n]
    return Job(kind, chunk, sum(k == "A" for k, _ in order[:n]), sum(k == "B" for k, _ in order[:n]), n % 2,
               job_at(n - 1))


JOBS = 2 * CHUNKS
LATE_STEPS = (1, JOBS - 2)
FRONT_LATE = 8


def loop_jobs(loop):
    jobs = []
    for kind, n, a, b in (("B", -1, 1, -1), ("A", 1, 1, 0), ("B", 0, 2, 0), ("A", 2, 2, 1), ("B", 1, 3, 1)):
        jobs.append(Job(kind, loop.c + n, a, b, "BA".index(kind), jobs[-1] if jobs else None, loop))
    return jobs


class Signal:

    def __init__(self, handle, per_a, per_b=None):
        self.handle, self.per_a = handle, per_a
        self.per_b = per_a if per_b is None else per_b

    def value(self, job, count):
        return job.a * self.per_a + job.b * self.per_b + count

    def wait(self, eng, job, count, apart=False):
        if job is None:
            return
        v = self.value(job, count)
        if job.loop:
            job.loop.wait_ge(self.handle, self.per_a + self.per_b, v, apart)
        elif v > 0:
            eng.wait_ge(self.handle, v)


def build(nc, x, w_qkv, w_o, g1, b1, wg, w1, bb1, w2, bb2, g2, b2, out):
    x_tiles = x.rearrange("(c q) (h p) d -> c p (q h) d", q=2, p=P)
    out_tiles = out.rearrange("(c q) (h p) d -> c p (q h) d", q=2, p=P)
    middle = nc.dram_tensor("after_first_ffn", [CHUNKS, P, TT, D], F32, kind="Internal").ap()

    with ExitStack() as ctx:
        def sb(name, shape, dt=F32):
            return ctx.enter_context(nc.sbuf_tensor(name, shape, dt))

        def sem(name):
            return ctx.enter_context(nc.semaphore(name))

        def signal(name, per_a, per_b=None):
            return Signal(sem(name), per_a, per_b)

        wqkv = sb("wqkv", [P, 3 * D])
        wo = sb("wo", [P, D])
        wgate = sb("wgate", [P, E])
        w1_hi, w1_lo = sb("w1_hi", [P, E, F], F32R), sb("w1_lo", [P, E, F], F32R)
        w2_hi, w2_lo = sb("w2_hi", [P, E, FC, D], F32R), sb("w2_lo", [P, E, FC, D], F32R)
        bb1_t = sb("bb1_t", [P, HID])
        bb2_twice = sb("bb2_twice", [2 * E, D])
        g1_col, b1_col = sb("g1_col", [P, 1]), sb("b1_col", [P, 1])
        g2_half, b2_half = sb("g2_half", [P, D]), sb("b2_half", [P, D])
        rows = sb("rows", [1, 2, D])
        ident = sb("ident", [P, P])
        ident_bf = sb("ident_bf", [P, P], BF16)
        causal = sb("causal", [P, 4, P], BF16)
        head_rows = sb("head_rows", [P, GROUPS])
        expert_no = sb("expert_no", [P, E])
        ones_row = sb("ones_row", [1, P])
        power = sb("power", [P, TT])
        phase_of = sb("phase_of", [P, RATE])
        shift_rows = sb("shift_rows", [P, 1])
        head_shift = sb("head_shift", [P, GROUPS])
        expert_rows = sb("expert_rows", [2 * E, E], F32R)

        xin = sb("xin", [P, TT, D])
        xn = sb("xn", [P, TT, 132])
        xn_t = sb("xn_t", [P, TOK])
        long_rec = sb("long_rec", [P, TT])
        qk = sb("qk", [P, 4, TOK], F32R)
        q4 = sb("q4", [P, GROUPS, TOK], F32R)
        k4 = sb("k4", [P, GROUPS * TOK])
        k_diag = sb("k_diag", [P, GROUPS, 4, TOK], F32R)
        values = sb("values", [P, TT, HEADS, SLOT])
        row_max = sb("row_max", [P, TT, HEADS])
        shift_hi = sb("shift_hi", [P, TT, HEADS], F32R)
        shift_cols = sb("shift_cols", [P, TT, GROUPS, 4, 8])
        attn_t = sb("attn_t", [P, GROUPS, S])
        denom = sb("denom", [P, TT, HEADS])
        attn = sb("attn", [P, TT, D])
        stats = sb("stats", [P, TT, 6])
        moments = sb("moments", [P, TT, 2])
        var_eps, rstd = sb("var_eps", [P, TT]), sb("rstd", [P, TT])
        logits = sb("logits", [P, TT, E])
        top8, top8_at = sb("top8", [P, TT, 8]), sb("top8_at", [P, TT, 8], U32)
        top_at = sb("top_at", [P, TT, 2])
        gap, gap_exp = sb("gap", [P, TT]), sb("gap_exp", [P, TT])
        gate_den = sb("gate_den", [P, TT])
        gates = sb("gates", [P, 2, TT])
        first_gate, second_gate = sb("first_gate", [P, TT, E]), sb("second_gate", [P, TT, E])
        gate_w = sb("gate_w", [P, TT, E])
        gate_hi = sb("gate_hi", [P, TT, E], F32R)
        gate_parts = sb("gate_parts", [P, TT, 2 * E])

        long_e = k4[:, 0:2 * 2 * S].rearrange("p (b k q) -> p b k q", b=2, k=2)
        probs = k4[:, 0:4 * 3 * P].rearrange("p (n c) -> p n c", n=4)
        attn_feat, mid = xn_t, attn

        k4_groups = k4[:, :].rearrange("p (j t) -> p j t", j=GROUPS)

        acc = sb("acc", [P, 2, TOK])
        h_hi, h_lo = sb("h_hi", [P, 2, TOK], F32R), sb("h_lo", [P, 2, TOK], F32R)
        gate_rows = sb("gate_rows", [2 * E, 2, TOK], F32R)
        x_plus = sb("x_plus", [P, 2, TT, D])

        act = sb("act", [P, 2, TOK])
        act_hi, act_lo = sb("act_hi", [P, 4, TOK], F32R), sb("act_lo", [P, 4, TOK], F32R)
        gate_bc = sb("gate_bc", [P, 2, TOK])
        gated = sb("gated", [P, 2, TOK])
        end_rows = sb("end_rows", [P, TT, D])
        end_norm = sb("end_norm", [P, TT, D])
        end_stats, end_moments = sb("end_stats", [P, TT, 6]), sb("end_moments", [P, TT, 2])
        end_var, end_rstd = sb("end_var", [P, TT]), sb("end_rstd", [P, TT])

        ps_hidden = ctx.enter_context(nc.psum_tensor("ps_hidden", [P, 2, 512], F32))
        ps_y = ctx.enter_context(nc.psum_tensor("ps_y", [P, 512], F32))
        ps_ring = ctx.enter_context(nc.psum_tensor("ps_ring", [P, RING, 512], F32))
        ps_attn = ctx.enter_context(nc.psum_tensor("ps_attn", [P, 512], F32))

        small_in = sem("small_in")
        weights_in = [sem(f"weights_in{i}") for i in range(2)]
        weights_hi, weights_lo = sem("weights_hi"), sem("weights_lo")
        const_dve, const_pool, const_mid = sem("const_dve"), sem("const_pool"), sem("const_mid")
        set_full, set_done = sem("set_full"), sem("set_done")

        x_in = signal("x_in", 16)
        norm_stats, norm_moments = signal("norm_stats", 2, 3), signal("norm_moments", 2, 3)
        norm_var, norm_rstd = signal("norm_var", 2, 3), signal("norm_rstd", 2, 3)
        xn_ready = signal("xn_ready", 1, 2)
        ring_full = signal("ring_full", len(RING_USES["A"]), len(RING_USES["B"]))
        ring_free = [signal(f"ring_free{i}", len(RING_USES["A"]) // RING, len(RING_USES["B"]) // RING)
                     for i in range(RING)]
        long_masked, long_full = signal("long_masked", 0, 2), signal("long_full", 0, 2)
        long_recip = signal("long_recip", 0, 2)
        attn_free = signal("attn_free", 4, 6)
        qk_hi = signal("qk_hi", 2)
        parts_in = signal("parts_in", 16 * 24)
        k_diag_ready = signal("k_diag_ready", 1)
        shift_hi_ready, shift_ready = signal("shift_hi_ready", 2), signal("shift_ready", 2)
        probs_ready, values_done = signal("probs_ready", 32), signal("values_done", 32)
        denom_ready = signal("denom_ready", 4)
        mid_ready = signal("mid_ready", 1)
        h_hi_ready, h_ready = signal("h_hi_ready", 1), signal("h_ready", 1)
        top_ready, top_at_ready, gap_ready = signal("top_ready", 1), signal("top_at_ready", 1), signal("gap_ready", 1)
        gap_exp_ready = signal("gap_exp_ready", 1)
        gate_step, gate_ready = signal("gate_step", 6), signal("gate_ready", 1)

        hidden_full, hidden_free = signal("hidden_full", HID + E), signal("hidden_free", HID + E)
        act_hi_ready, act_ready = signal("act_hi_ready", HID), signal("act_ready", HID)
        act_used = signal("act_used", HID)
        bias_full = signal("bias_full", 1)
        y_free = signal("y_free", E + 2)
        added = signal("added", E)
        turned = signal("turned", 1)
        end_stats_in, end_moments_in = signal("end_stats_in", 1), signal("end_moments_in", 1)
        end_var_in, end_rstd_in = signal("end_var_in", 1), signal("end_rstd_in", 1)
        end_normed, end_scaled = signal("end_normed", 1), signal("end_scaled", 1)
        result_ready, stored = signal("result_ready", 1), signal("stored", 16)

        def ring_bank(job, use):
            return ps_ring[:, RING_USES[job.kind][use] % RING, :]

        def wait_bank(eng, job, use):
            n = RING_USES[job.kind][use]
            ring_free[n % RING].wait(eng, job, n // RING)

        def wait_filled(eng, job, use):
            ring_full.wait(eng, job, RING_USES[job.kind][use] + 1)

        def emptied(job, use):
            return ring_free[RING_USES[job.kind][use] % RING].handle

        def wait_emptied(eng, job, use, apart=False):
            n = RING_USES[job.kind][use]
            ring_free[n % RING].wait(eng, job, n // RING + 1, apart)

        def hidden_use(t):
            return t + (t + FC - 1) // FC

        def gates_use(e):
            return hidden_use(FC * e) + 1

        def norm_no(job, which):
            return NORMS[job.kind].index(which)

        def on_ticks(engine_front, engine_middle, engine_end, middle, front, end, s, setup=None):
            late = FRONT_LATE if s in LATE_STEPS else 0
            for t in range(TICKS + late):
                if middle and t < TICKS:
                    engine_middle(middle, t)
                if end and t < TICKS:
                    engine_end(end, t)
                if setup and t % 2 == 0 and t // 2 < E:
                    setup(t // 2)
                if front and t >= late:
                    for piece in front_pieces(front.kind, t - late):
                        engine_front(front, *piece)

        def run_steps(eng, one_step):
            for s in range(-1, 3):
                one_step(job_at(s), job_at(s + 1), job_at(s - 1), job_at(s + 2), s)
            with eng.Fori(1, CHUNKS - 2) as c:
                jobs = loop_jobs(LoopCount(eng, c, eng is nc.sync, const_dve))
                one_step(jobs[1], jobs[2], jobs[0], jobs[3], None)
                one_step(jobs[2], jobs[3], jobs[1], jobs[4], None)
            for s in range(JOBS - 3, JOBS + 1):
                one_step(job_at(s), job_at(s + 1), job_at(s - 1), job_at(s + 2), s)

        stage = [k4[:, 0:2 * F], k4[:, 2 * F:4 * F]]
        bb1_rows = end_rows[0:HID, 0, :]

        CONSTANTS = 4

        block = ctx.enter_context(nc.Block())

        @block.sync
        def _(sp):
            def load(job):
                xn_ready.wait(sp, job, 0)
                if job.kind == "B":
                    before = job.b if not job.loop and job.b == 0 else job.b - 1
                    stored.wait(sp, Job("A", job.chunk, job.b, before, 0, loop=job.loop), 16)
                source = x_tiles if job.kind == "A" else middle
                sp.dma_start(xin[:, :, :], source[job.chunk]).then_inc(x_in.handle, 16)

            def spread(job):
                ring_full.wait(sp, job, 0)
                k_diag_ready.wait(sp, job, 0)
                wait_emptied(sp, job, ("queries_keys", 1))
                wait_emptied(sp, job, ("queries_keys", 0))
                if job.kind == "A" and isinstance(job.chunk, int) and job.chunk == 0:
                    sp.wait_ge(weights_lo, E)
                for of, to, parts in ((2, k4_groups, (0, 1, 0)), (0, q4[:, :, :].bitcast(F32), (0, 0, 1))):
                    for row, part in enumerate(parts):
                        for j in range(GROUPS):
                            sp.dma_start(to[32 * row:32 * row + 32, j, :],
                                         qk[32 * j:32 * j + 32, of + part, :].bitcast(F32)
                                         ).then_inc(parts_in.handle, 16)

            def store(job):
                result_ready.wait(sp, job, 1)
                target = middle if job.kind == "A" else out_tiles
                sp.dma_start(target[job.chunk], end_norm[:, :, :]).then_inc(stored.handle, 16)

            def load_expert(e):
                if e >= 2:
                    sp.wait_ge(weights_hi, e - 1)
                    sp.wait_ge(weights_lo, e - 1)
                sp.dma_start(stage[e % 2][:, 0:F], w1[e]).then_inc(weights_in[e % 2], 16)
                sp.dma_start(stage[e % 2][:, F:2 * F].rearrange("p (c n) -> p c n", c=FC),
                             w2[e].rearrange("(c p) n -> p c n", p=P)).then_inc(weights_in[e % 2], 16)

            sp.dma_start(wqkv[:, :], w_qkv).then_inc(small_in, 16)
            sp.dma_start(wo[:, :], w_o).then_inc(small_in, 16)
            sp.dma_start(wgate[:, :], wg).then_inc(small_in, 16)
            sp.dma_start(g1_col[:, :], g1.rearrange("(p a) -> p a", a=1)).then_inc(small_in, 16)
            sp.dma_start(b1_col[:, :], b1.rearrange("(p a) -> p a", a=1)).then_inc(small_in, 16)
            sp.dma_start(rows[:, 0, :], g2.rearrange("(a n) -> a n", a=1)).then_inc(small_in, 16)
            sp.dma_start(rows[:, 1, :], b2.rearrange("(a n) -> a n", a=1)).then_inc(small_in, 16)
            sp.dma_start(bb2_twice[0:E, :], bb2).then_inc(small_in, 16)
            sp.dma_start(bb2_twice[E:2 * E, :], bb2).then_inc(small_in, 16)
            sp.dma_start(bb1_rows, bb1.rearrange("e (c p) -> (e c) p", p=P)).then_inc(small_in, 16)

            def step(mid_job, front_job, end_job, next_job, s):
                if s == -1:
                    load(front_job)
                    for e in range(E):
                        load_expert(e)
                if end_job:
                    store(end_job)
                if s in LATE_STEPS:
                    load(front_job)
                if front_job:
                    spread(front_job)
                if next_job and (s is None or s + 1 not in LATE_STEPS):
                    load(next_job)

            run_steps(sp, step)
            stored.wait(sp, Job("B", 0, CHUNKS, CHUNKS, 0), 0)

        @block.tensor
        def _(pe):
            def front(job, piece, *at):
                use = (piece,) + at
                if piece in ("long_turn", "turn"):
                    xn_ready.wait(pe, job, 1 if piece == "long_turn" or job.kind == "A" else 2)
                    wait_bank(pe, job, use)
                    for n in range(2):
                        mm = pe.transpose(ring_bank(job, use)[:, n * P:(n + 1) * P], xn[:, 2 * at[0] + n, 0:D],
                                          ident[:, :])
                    mm.then_inc(ring_full.handle, 1)
                elif piece == "long_scores":
                    b, = at
                    wait_emptied(pe, job, ("long_turn", b))
                    wait_bank(pe, job, use)
                    for kt in range(2):
                        mm = pe.matmul(ring_bank(job, use)[:, kt * S:(kt + 1) * S],
                                       xn_t[:, b * S + kt * P:b * S + (kt + 1) * P], xn_t[:, b * S:(b + 1) * S],
                                       start=True, stop=True)
                    mm.then_inc(ring_full.handle, 1)
                elif piece == "long_values":
                    b, = at
                    long_masked.wait(pe, job, b + 1)
                    attn_free.wait(pe, job, b)
                    for qt in range(2):
                        for kt in range(2):
                            mm = pe.matmul(ps_attn[:, qt * S:qt * S + D + 1],
                                           long_e[:, b, kt, qt * P:(qt + 1) * P], xn[:, 2 * b + kt, 0:D + 1],
                                           start=(kt == 0), stop=(kt == 1))
                    mm.then_inc(long_full.handle, 1)
                elif piece == "queries_keys":
                    which, = at
                    wait_emptied(pe, job, ("turn", 0))
                    wait_emptied(pe, job, ("turn", 1))
                    wait_bank(pe, job, use)
                    pe.matmul(ring_bank(job, use), wqkv[:, which * D:(which + 1) * D], xn_t[:, :],
                              start=True, stop=True).then_inc(ring_full.handle, 1)
                elif piece == "project_values":
                    wait_bank(pe, job, use)
                    for tt in range(TT):
                        mm = pe.matmul(ring_bank(job, use)[:, tt * P:(tt + 1) * P], xn_t[:, tt * P:(tt + 1) * P],
                                       wqkv[:, 2 * D:3 * D], start=True, stop=True)
                    mm.then_inc(ring_full.handle, 1)
                elif piece == "scores":
                    b, j = at
                    if at == (0, 0):
                        parts_in.wait(pe, job, 16 * 24)
                        k_diag_ready.wait(pe, job, 1)
                    for part in range(3):
                        key = use + (part,)
                        wait_bank(pe, job, key)
                        bank = ring_bank(job, key)
                        if part == 0:
                            pe.matmul(bank, q4[0:96, j, b * S:b * S + P],
                                      k_diag[0:96, j, :, b * S:b * S + P], start=True, stop=False)
                            mm = pe.matmul(bank, ident_bf[:, :], causal[:, :, :], start=False, stop=True)
                        else:
                            i = 2 * (part - 1)
                            pe.matmul(bank, q4[0:96, j, b * S + P:(b + 1) * S],
                                      k_diag[0:96, j, i:i + 2, b * S:(b + 1) * S], start=True, stop=False)
                            mm = pe.matmul(bank.rearrange("p (i k) -> p i k", i=2)[:, :, P:S], ident_bf[:, :],
                                           causal[:, 0:2, :], start=False, stop=True)
                        mm.then_inc(ring_full.handle, 1)
                elif piece == "shift":
                    b, = at
                    shift_ready.wait(pe, job, b + 1)
                    wait_bank(pe, job, use)
                    for n in range(2):
                        mm = pe.transpose(ring_bank(job, use)[:, n * P:(n + 1) * P],
                                          shift_cols[:, 2 * b + n, :, :, :].rearrange("p j i c -> p (j i c)"),
                                          ident[:, :])
                    mm.then_inc(ring_full.handle, 1)
                elif piece == "head":
                    k, = at
                    b, j, i = k // HEADS, k % HEADS // 4, k % 4
                    if k % HEADS == 0:
                        wait_emptied(pe, job, ("shift", b))
                    wait_bank(pe, job, use)
                    bank = ring_bank(job, use)
                    pe.matmul(bank[:, 0:S], k_diag[:, j, i, b * S + P:(b + 1) * S],
                              q4[:, j, b * S:(b + 1) * S], start=True, stop=True)
                    pe.matmul(bank[:, S:2 * S], k_diag[:, j, i, b * S:b * S + P],
                              q4[:, j, b * S:(b + 1) * S], start=True, stop=True
                              ).then_inc(ring_full.handle, 1)
                    if k >= VLAG:
                        head_values(job, k - VLAG)
                    if k == 2 * HEADS - 1:
                        for late in range(k - VLAG + 1, 2 * HEADS):
                            head_values(job, late)
                elif piece == "rows":
                    b, qt = at
                    attn_free.wait(pe, job, (2 if job.kind == "B" else 0) + 2 * b + 2)
                    wait_bank(pe, job, use)
                    for j in range(GROUPS):
                        mm = pe.transpose(ring_bank(job, use)[:, j * P:(j + 1) * P],
                                          attn_t[:, j, qt * P:(qt + 1) * P], ident[:, :])
                    mm.then_inc(ring_full.handle, 1)
                elif piece == "merge":
                    for b in range(2):
                        for qt in range(2):
                            wait_emptied(pe, job, ("rows", b, qt))
                    wait_bank(pe, job, use)
                    for tt in range(TT):
                        mm = pe.transpose(ring_bank(job, use)[:, tt * P:(tt + 1) * P], attn[:, tt, :], ident[:, :])
                    mm.then_inc(ring_full.handle, 1)
                elif piece == "attn_out":
                    wait_emptied(pe, job, ("merge",))
                    wait_bank(pe, job, use)
                    for tt in range(TT):
                        mm = pe.matmul(ring_bank(job, use)[:, tt * P:(tt + 1) * P],
                                       attn_feat[:, tt * P:(tt + 1) * P], wo[:, :], start=True, stop=True)
                    mm.then_inc(ring_full.handle, 1)
                elif piece == "hidden":
                    mid_ready.wait(pe, job, 1)
                    wait_bank(pe, job, use)
                    for tt in range(TT):
                        mm = pe.transpose(ring_bank(job, use)[:, tt * P:(tt + 1) * P], mid[:, tt, :], ident[:, :])
                    mm.then_inc(ring_full.handle, 1)
                elif piece == "route":
                    wait_emptied(pe, job, ("hidden",))
                    wait_bank(pe, job, use)
                    for tt in range(TT):
                        mm = pe.matmul(ring_bank(job, use)[:, tt * E:(tt + 1) * E],
                                       acc[:, job.parity, tt * P:(tt + 1) * P], wgate[:, :], start=True, stop=True)
                    mm.then_inc(ring_full.handle, 1)
                elif piece == "gate_turn":
                    gate_ready.wait(pe, job, 1)
                    wait_bank(pe, job, use)
                    for tt in range(TT):
                        mm = pe.transpose(ring_bank(job, use)[0:2 * E, tt * P:(tt + 1) * P], gate_parts[:, tt, :],
                                          ident[:, :])
                    mm.then_inc(ring_full.handle, 1)

            def head_values(job, k):
                b, j, i = k // HEADS, k % HEADS // 4, k % 4
                if k == 0:
                    wait_emptied(pe, job, ("project_values",))
                if k % 8 == 0:
                    attn_free.wait(pe, job, (2 if job.kind == "B" else 0) + k // 8)
                probs_ready.wait(pe, job, k + 1)
                to = ps_attn[32 * i:32 * i + SLOT, (j % 2) * S:(j % 2 + 1) * S]
                pe.matmul(to, values[:, 2 * b, 4 * j + i, :], probs[:, k % 4, P:3 * P], start=True, stop=False,
                          tile_position=(0, 32 * i))
                pe.matmul(to[:, P:S], values[:, 2 * b + 1, 4 * j + i, :], probs[:, k % 4, 0:P], start=False,
                          stop=True, tile_position=(0, 32 * i)).then_inc(values_done.handle, 1)

            def middle_tick(job, t):
                if t < HID:
                    e, f = t // FC, t % FC
                    if t == 0:
                        h_ready.wait(pe, job, 1)
                    if f == 1:
                        n = gates_use(e)
                        if e == 0:
                            wait_emptied(pe, job, ("gate_turn",))
                        hidden_free.wait(pe, job, n - 1)
                        pe.matmul(ps_hidden[:, n % 2, :], expert_rows[:, e:e + 1].broadcast_to([2 * E, P]), gate_rows[:, job.parity, :],
                                  start=True, stop=True).then_inc(hidden_full.handle, 1)
                    n = hidden_use(t)
                    hidden_free.wait(pe, job, n - 1)
                    to, cols = ps_hidden[:, n % 2, :], slice(f * P, (f + 1) * P)
                    pe.matmul(to, w1_hi[:, e, cols], h_hi[:, job.parity, :], start=True, stop=False)
                    pe.matmul(to, w1_hi[:, e, cols], h_lo[:, job.parity, :], start=False, stop=False)
                    pe.matmul(to, w1_lo[:, e, cols], h_hi[:, job.parity, :], start=False, stop=True
                              ).then_inc(hidden_full.handle, 1)
                if t == 2:
                    y_free.wait(pe, job, 0)
                    pe.matmul(ps_y[:, :], bb2_twice[:, :], gate_rows[:, job.parity, :].bitcast(F32),
                              start=True, stop=True).then_inc(bias_full.handle, 1)
                if t >= LAG:
                    u = t - LAG
                    e, f = u // FC, u % FC
                    if f == 0:
                        y_free.wait(pe, job, e + 1)
                    act_ready.wait(pe, job, u + 1)
                    pe.matmul(ps_y[:, :], w2_hi[:, e, f, :], act_hi[:, u % 4, :], start=(f == 0), stop=False)
                    pe.matmul(ps_y[:, :], w2_hi[:, e, f, :], act_lo[:, u % 4, :], start=False, stop=False)
                    pe.matmul(ps_y[:, :], w2_lo[:, e, f, :], act_hi[:, u % 4, :], start=False, stop=(f == FC - 1)
                              ).then_inc(act_used.handle, 1)

            def end_tick(job, t):
                if t == 0:
                    added.wait(pe, job, E)
                    y_free.wait(pe, job, E + 1)
                    for tt in range(TT):
                        mm = pe.transpose(ps_y[:, tt * P:(tt + 1) * P], acc[:, job.parity, tt * P:(tt + 1) * P],
                                          ident[:, :])
                    mm.then_inc(turned.handle, 1)

            pe.wait_ge(small_in, 16 * 10)
            pe.wait_ge(const_pool, 3)
            pe.wait_ge(const_dve, CONSTANTS)
            pe.matmul(ps_attn[:, 0:2 * D], ones_row[:, :], rows[:, :, :], start=True, stop=True)
            pe.transpose(ps_attn[:, 2 * D:2 * D + HID], bb1_rows, ident[0:HID, 0:HID]).then_inc(set_full, 1)

            def step(mid_job, front_job, end_job, next_job, s):
                if s == 0:
                    pe.wait_ge(weights_hi, E)
                    pe.wait_ge(weights_lo, E)
                if s == -1:
                    pe.wait_ge(set_done, 1)
                on_ticks(front, middle_tick, end_tick, mid_job, front_job, end_job, s)

            run_steps(pe, step)

        @block.scalar
        def _(act_eng):
            sc = act_eng

            def front(job, piece, *at):
                use = (piece,) + at
                if piece in ("long_turn", "turn"):
                    wait_filled(sc, job, use)
                    sc.activation(xn_t[:, at[0] * S:(at[0] + 1) * S], ring_bank(job, use)[:, 0:S], ACT.Copy
                                  ).then_inc(emptied(job, use), 1)
                elif piece == "long_scores":
                    wait_filled(sc, job, use)
                    sc.activation(long_e[:, at[0], :, :].rearrange("p k q -> p (k q)"), ring_bank(job, use),
                                  ACT.Exp, scale=D ** -0.5).then_inc(emptied(job, use), 1)
                elif piece == "queries_keys":
                    parts_in.wait(sc, job, 0)
                    wait_filled(sc, job, use)
                    sc.activation(qk[:, 2 * at[0], :], ring_bank(job, use), ACT.Copy).then_inc(qk_hi.handle, 1)
                elif piece == "project_values":
                    wait_filled(sc, job, use)
                    sc.activation(values[:, :, :, 0:HD],
                                  ring_bank(job, use).rearrange("p (t h d) -> p t h d", t=TT, h=HEADS), ACT.Copy
                                  ).then_inc(emptied(job, use), 1)
                elif piece == "shift":
                    b, = at
                    wait_filled(sc, job, use)
                    for j in range(GROUPS):
                        ins = sc.activation(q4[96:128, j, b * S:(b + 1) * S],
                                            ring_bank(job, use)[32 * j:32 * j + 32, 0:S], ACT.Copy)
                    ins.then_inc(emptied(job, use), 1)
                elif piece == "head":
                    k, = at
                    values_done.wait(sc, job, k - 3)
                    wait_filled(sc, job, use)
                    sc.activation(probs[:, k % 4, :], ring_bank(job, use)[:, P:4 * P], ACT.Exp, scale=HD ** -0.5
                                  ).then_inc(emptied(job, use), 1)
                    if k % 8 == VLAG and k > 8:
                        attn_copy(job, k // 8 - 1)
                    if k == 2 * HEADS - 1:
                        attn_copy(job, 3)
                elif piece == "merge":
                    wait_filled(sc, job, use)
                    sc.activation(attn_feat[:, :], ring_bank(job, use), ACT.Copy).then_inc(emptied(job, use), 1)
                elif piece == "hidden":
                    turned.wait(sc, job.before, 0)
                    wait_filled(sc, job, use)
                    sc.activation(acc[:, job.parity, :], ring_bank(job, use), ACT.Identity, bias=b1_col[:, 0:1],
                                  scale=g1_col[:, 0:1]).then_inc(emptied(job, use), 1)
                elif piece == "gate":
                    gap_ready.wait(sc, job, 1)
                    sc.activation(gap_exp[:, :], gap[:, :], ACT.Exp).then_inc(gap_exp_ready.handle, 1)
                elif piece == "gate_turn":
                    wait_filled(sc, job, use)
                    sc.activation(gate_rows[:, job.parity, :], ring_bank(job, use)[0:2 * E, :], ACT.Copy
                                  ).then_inc(emptied(job, use), 1)

            def attn_copy(job, n):
                values_done.wait(sc, job, 8 * n + 8)
                if n == 2:
                    wait_filled(sc, job, ("rows", 0, 1))
                sc.activation(attn_t[:, 2 * (n % 2):2 * (n % 2) + 2, :].rearrange("p j q -> p (j q)"),
                              ps_attn[:, :], ACT.Copy).then_inc(attn_free.handle, 1)

            def middle_tick(job, t):
                if t >= HID:
                    return
                e, f = t // FC, t % FC
                if f == 1:
                    n = gates_use(e)
                    hidden_full.wait(sc, job, n + 1)
                    if e >= 2:
                        y_free.wait(sc, job, e)
                    sc.activation(gate_bc[:, e % 2, :], ps_hidden[:, n % 2, :], ACT.Copy
                                  ).then_inc(hidden_free.handle, 1)
                n = hidden_use(t)
                act_ready.wait(sc, job, t - 1)
                hidden_full.wait(sc, job, n + 1)
                sc.activation(act[:, t % 2, :], ps_hidden[:, n % 2, :], ACT.Gelu_apprx_tanh, bias=bb1_t[:, t:t + 1]
                              ).then_inc(hidden_free.handle, 1)

            def end_tick(job, t):
                if t == 1:
                    turned.wait(sc, job, 1)
                    sc.activation(end_rows[:, :, :].rearrange("p t d -> p (t d)"), ps_y[:, :], ACT.Copy
                                  ).then_inc(y_free.handle, 1)

            def split_expert(e):
                sc.wait_ge(weights_in[e % 2], 32 * (e // 2 + 1))
                sc.activation(w1_hi[:, e, :], stage[e % 2][:, 0:F], ACT.Copy)
                sc.activation(w2_hi[:, e, :, :].rearrange("p c n -> p (c n)"), stage[e % 2][:, F:2 * F], ACT.Copy
                              ).then_inc(weights_hi, 1)

            sc.wait_ge(set_full, 1)
            sc.activation(g2_half[:, :], ps_attn[:, 0:D], ACT.Copy, scale=0.5)
            sc.activation(b2_half[:, :], ps_attn[:, D:2 * D], ACT.Copy, scale=0.5)
            sc.activation(bb1_t[:, :], ps_attn[:, 2 * D:2 * D + HID], ACT.Copy).then_inc(set_done, 1)

            def step(mid_job, front_job, end_job, next_job, s):
                if s == 0:
                    sc.wait_ge(weights_lo, E)
                on_ticks(front, middle_tick, end_tick, mid_job, front_job, end_job, s,
                         split_expert if s == -1 else None)

            run_steps(sc, step)

        @block.vector
        def _(dve):
            def norm_statistics(job, which, rows_of, width_ok=True):
                n = norm_no(job, which)
                for tt in range(TT):
                    ins = dve.bn_stats(stats[:, tt, :], rows_of(tt))
                ins.then_inc(norm_stats.handle, 1)
                norm_stats.wait(dve, job, n + 1, apart=True)
                for tt in range(TT):
                    ins = dve.bn_aggr(moments[:, tt, :], stats[:, tt, :])
                ins.then_inc(norm_moments.handle, 1)
                norm_moments.wait(dve, job, n + 1)
                dve.tensor_scalar(var_eps[:, :], moments[:, :, 1], EPS, None, ALU.add).then_inc(norm_var.handle, 1)

            def normalise(job, which, to, rows_of):
                norm_rstd.wait(dve, job, norm_no(job, which) + 1)
                for tt in range(TT):
                    ins = dve.tensor_scalar(to(tt), rows_of(tt), moments[:, tt, 0:1], rstd[:, tt:tt + 1],
                                            ALU.subtract, ALU.mult)
                return ins

            def front(job, piece, *at):
                use = (piece,) + at
                if piece == "long_stats":
                    x_in.wait(dve, job, 16)
                    norm_statistics(job, "long", lambda tt: xin[:, tt, :])
                elif piece == "long_norm":
                    normalise(job, "long", lambda tt: xn[:, tt, 0:D], lambda tt: xin[:, tt, :]
                              ).then_inc(xn_ready.handle, 1)
                elif piece == "long_values":
                    b, = at
                    long_full.wait(dve, job, b + 1)
                    pair = ps_attn[:, :].rearrange("p (q n) -> p q n", q=2)
                    dve.reciprocal(long_rec[:, 2 * b:2 * b + 2], pair[:, :, D]).then_inc(long_recip.handle, 1)
                    long_recip.wait(dve, job, b + 1)
                    for qt in range(2):
                        tt = 2 * b + qt
                        ins = dve.scalar_tensor_tensor(out=xin[:, tt, :], in0=pair[:, qt, 0:D],
                                                       scalar=long_rec[:, tt:tt + 1], in1=xin[:, tt, :],
                                                       op0=ALU.mult, op1=ALU.add)
                    ins.then_inc(attn_free.handle, 1)
                elif piece == "stats":
                    if job.kind == "A":
                        x_in.wait(dve, job, 16)
                    else:
                        attn_free.wait(dve, job, 2)
                    norm_statistics(job, "norm", lambda tt: xin[:, tt, :])
                    dve.tensor_tensor(x_plus[:, job.parity, :, :], xin[:, :, :],
                                      b2_half[:, :].unsqueeze(1).broadcast_to([P, TT, D]), ALU.add)
                elif piece == "norm":
                    normalise(job, "norm", lambda tt: xn[:, tt, 0:D], lambda tt: xin[:, tt, :]
                              ).then_inc(xn_ready.handle, 1)
                elif piece == "queries_keys":
                    which, = at
                    qk_hi.wait(dve, job, 2 - which)
                    dve.tensor_tensor(qk[:, 2 * which + 1, :], ring_bank(job, use), qk[:, 2 * which, :].bitcast(F32),
                                      ALU.subtract).then_inc(emptied(job, use), 1)
                elif piece == "scores":
                    b, j = at
                    for part in range(3):
                        key = use + (part,)
                        wait_filled(dve, job, key)
                        if part == 0:
                            to, n = row_max[:, 2 * b, 4 * j:4 * j + 4], 4
                        else:
                            i = 4 * j + 2 * (part - 1)
                            to, n = row_max[:, 2 * b + 1, i:i + 2], 2
                        dve.tensor_reduce(to, ring_bank(job, key).rearrange("p (i k) -> p i k", i=n), AX.X, ALU.max
                                          ).then_inc(emptied(job, key), 1)
                elif piece == "shift":
                    b, = at
                    wait_emptied(dve, job, ("scores", b, GROUPS - 1, 2))
                    high, low = shift_hi[:, 2 * b:2 * b + 2, :], row_max[:, 2 * b:2 * b + 2, :]
                    dve.tensor_scalar(high, low, -1.0, None, ALU.mult).then_inc(shift_hi_ready.handle, 1)
                    shift_hi_ready.wait(dve, job, b + 1)
                    cols = shift_cols[:, 2 * b:2 * b + 2, :, :, :].rearrange("p t j i c -> p t (j i) c")
                    dve.tensor_copy(cols[:, :, :, 0], high.bitcast(F32))
                    dve.scalar_tensor_tensor(out=cols[:, :, :, 1], in0=low, scalar=-1.0, in1=high.bitcast(F32),
                                             op0=ALU.mult, op1=ALU.subtract).then_inc(shift_ready.handle, 1)
                elif piece == "rows":
                    b, qt = at
                    tt = 2 * b + qt
                    wait_filled(dve, job, use)
                    heads = ring_bank(job, use).rearrange("p (h c) -> p h c", h=HEADS)
                    dve.reciprocal(denom[:, tt, :], heads[:, :, HD]).then_inc(denom_ready.handle, 1)
                    denom_ready.wait(dve, job, tt + 1)
                    dve.tensor_tensor(attn[:, tt, :].rearrange("p (h d) -> p h d", h=HEADS), heads[:, :, 0:HD],
                                      denom[:, tt, :].unsqueeze(2).broadcast_to([P, HEADS, HD]), ALU.mult
                                      ).then_inc(emptied(job, use), 1)
                elif piece == "attn_out":
                    wait_filled(dve, job, use)
                    dve.tensor_tensor(mid[:, :, :], ring_bank(job, use).rearrange("p (t d) -> p t d", t=TT),
                                      xn[:, :, 0:D], ALU.add).then_inc(emptied(job, use), 1)
                elif piece == "hidden_stats":
                    wait_emptied(dve, job, ("attn_out",))
                    norm_statistics(job, "hidden", lambda tt: mid[:, tt, :])
                elif piece == "hidden_norm":
                    normalise(job, "hidden", lambda tt: mid[:, tt, :], lambda tt: mid[:, tt, :]
                              ).then_inc(mid_ready.handle, 1)
                elif piece == "split_hidden":
                    act_used.wait(dve, job.before, 0)
                    wait_emptied(dve, job, ("hidden",))
                    dve.tensor_copy(h_hi[:, job.parity, :], acc[:, job.parity, :]).then_inc(h_hi_ready.handle, 1)
                    h_hi_ready.wait(dve, job, 1)
                    dve.tensor_tensor(h_lo[:, job.parity, :], acc[:, job.parity, :],
                                      h_hi[:, job.parity, :].bitcast(F32), ALU.subtract
                                      ).then_inc(h_ready.handle, 1)
                elif piece == "route":
                    wait_filled(dve, job, use)
                    dve.tensor_copy(logits[:, :, :], ring_bank(job, use)[:, 0:TT * E].rearrange(
                        "p (t e) -> p t e", t=TT)).then_inc(emptied(job, use), 1)
                    wait_emptied(dve, job, use, apart=True)
                    for tt in range(TT):
                        ins = dve.max(top8[:, tt, :], logits[:, tt, :])
                    ins.then_inc(top_ready.handle, 1)
                    top_ready.wait(dve, job, 1)
                    dve.tensor_tensor(gap[:, :], top8[:, :, 1], top8[:, :, 0], ALU.subtract
                                      ).then_inc(gap_ready.handle, 1)
                    for tt in range(TT):
                        ins = dve.max_index(top8_at[:, tt, :], top8[:, tt, :], logits[:, tt, :])
                    ins.then_inc(top_at_ready.handle, 1)
                elif piece == "gate":
                    top_at_ready.wait(dve, job, 1)
                    dve.tensor_copy(top_at[:, :, :], top8_at[:, :, 0:2])
                    gap_exp_ready.wait(dve, job, 1)
                    dve.tensor_scalar(gate_den[:, :], gap_exp[:, :], 1.0, None, ALU.add).then_inc(gate_step.handle, 1)
                    gate_step.wait(dve, job, 1)
                    dve.reciprocal(gates[:, 0, :], gate_den[:, :]).then_inc(gate_step.handle, 1)
                    gate_step.wait(dve, job, 2)
                    dve.tensor_tensor(gates[:, 1, :], gates[:, 0, :], gap_exp[:, :], ALU.mult
                                      ).then_inc(gate_step.handle, 1)
                    gate_step.wait(dve, job, 3)
                    for to, n in ((first_gate, 0), (second_gate, 1)):
                        for tt in range(TT):
                            ins = dve.tensor_scalar(to[:, tt, :], expert_no[:, :], top_at[:, tt, n:n + 1],
                                                    gates[:, n, tt:tt + 1], ALU.is_equal, ALU.mult)
                    ins.then_inc(gate_step.handle, 1)
                    gate_step.wait(dve, job, 4)
                    dve.tensor_tensor(gate_w[:, :, :], first_gate[:, :, :], second_gate[:, :, :], ALU.add
                                      ).then_inc(gate_step.handle, 1)
                    gate_step.wait(dve, job, 5)
                    dve.tensor_copy(gate_hi[:, :, :], gate_w[:, :, :]).then_inc(gate_step.handle, 1)
                    gate_step.wait(dve, job, 6)
                    dve.tensor_copy(gate_parts[:, :, 0:E], gate_hi[:, :, :].bitcast(F32))
                    dve.tensor_tensor(gate_parts[:, :, E:2 * E], gate_w[:, :, :], gate_hi[:, :, :].bitcast(F32),
                                      ALU.subtract).then_inc(gate_ready.handle, 1)

            def middle_tick(job, t):
                if t < HID:
                    hidden_free.wait(dve, job, hidden_use(t) + 1)
                    act_used.wait(dve, job, t - 3)
                    dve.tensor_copy(act_hi[:, t % 4, :], act[:, t % 2, :]).then_inc(act_hi_ready.handle, 1)
                    act_hi_ready.wait(dve, job, t + 1)
                    dve.tensor_tensor(act_lo[:, t % 4, :], act[:, t % 2, :], act_hi[:, t % 4, :].bitcast(F32),
                                      ALU.subtract).then_inc(act_ready.handle, 1)
                if t == 3:
                    bias_full.wait(dve, job, 1)
                    dve.tensor_tensor(acc[:, job.parity, :], ps_y[:, :], acc[:, job.parity, :], ALU.add
                                      ).then_inc(y_free.handle, 1)
                if t >= LAG and (t - LAG) % FC == FC - 1:
                    e = (t - LAG) // FC
                    hidden_free.wait(dve, job, gates_use(e) + 1)
                    act_used.wait(dve, job, FC * (e + 1))
                    if e >= 2:
                        added.wait(dve, job, e - 1)
                    elif e == 0:
                        added.wait(dve, job, 0)
                    dve.tensor_tensor(gated[:, e % 2, :], ps_y[:, :], gate_bc[:, e % 2, :], ALU.mult
                                      ).then_inc(y_free.handle, 1)

            def end_tick(job, t):
                if t == 2:
                    y_free.wait(dve, job, E + 2)
                    for tt in range(TT):
                        ins = dve.bn_stats(end_stats[:, tt, :], end_rows[:, tt, :])
                    ins.then_inc(end_stats_in.handle, 1)
                    end_stats_in.wait(dve, job, 1, apart=True)
                    for tt in range(TT):
                        ins = dve.bn_aggr(end_moments[:, tt, :], end_stats[:, tt, :])
                    ins.then_inc(end_moments_in.handle, 1)
                    end_moments_in.wait(dve, job, 1)
                    dve.tensor_scalar(end_var[:, :], end_moments[:, :, 1], EPS, None, ALU.add
                                      ).then_inc(end_var_in.handle, 1)
                if t == 4:
                    end_rstd_in.wait(dve, job, 1)
                    stored.wait(dve, job, 0)
                    for tt in range(TT):
                        ins = dve.tensor_scalar(end_norm[:, tt, :], end_rows[:, tt, :], end_moments[:, tt, 0:1],
                                                end_rstd[:, tt:tt + 1], ALU.subtract, ALU.mult)
                    ins.then_inc(end_normed.handle, 1)
                if t == 6:
                    end_scaled.wait(dve, job, 1)
                    dve.tensor_tensor(end_norm[:, :, :], end_norm[:, :, :], x_plus[:, job.parity, :, :], ALU.add
                                      ).then_inc(result_ready.handle, 1)

            def split_expert(e):
                dve.wait_ge(weights_hi, e + 1)
                dve.tensor_tensor(w1_lo[:, e, :], stage[e % 2][:, 0:F], w1_hi[:, e, :].bitcast(F32), ALU.subtract)
                dve.tensor_tensor(w2_lo[:, e, :, :].rearrange("p c n -> p (c n)"), stage[e % 2][:, F:2 * F],
                                  w2_hi[:, e, :, :].rearrange("p c n -> p (c n)").bitcast(F32), ALU.subtract
                                  ).then_inc(weights_lo, 1)

            dve.memset(values[:, :, :, :], 0.0).then_inc(const_dve, 1)
            dve.memset(shift_cols[:, :, :, :, :], 0.0)
            dve.memset(xn[:, :, D:D + 1], float(RATE))
            dve.memset(power[:, :], -0.5)
            dve.memset(ones_row[:, :], 1.0)
            for e in range(E):
                dve.memset(expert_no[:, e:e + 1], float(e))
            dve.wait_ge(const_dve, 1)
            dve.memset(values[:, :, :, HD:HD + 1], 1.0)
            dve.wait_ge(const_pool, 2)
            dve.tensor_copy(ident_bf[:, :], ident[:, :])
            dve.tensor_reduce(phase_of[:, :], ident[:, :].rearrange("p (m r) -> p r m", r=RATE), AX.X, ALU.add)
            dve.tensor_reduce(head_rows[:, :], ident[:, :].rearrange("p (a i d) -> p i a d", a=4, i=4), AX.XY,
                              ALU.add)
            dve.tensor_reduce(shift_rows[:, :], ident[:, :].rearrange("p (a d) -> p a d", d=8)[:, :, 0:2], AX.XY,
                              ALU.add)
            dve.tensor_tensor(expert_rows[:, :], ident[0:2 * E, 0:E], ident[0:2 * E, E:2 * E], ALU.add
                              ).then_inc(const_dve, 1)
            dve.wait_ge(const_dve, 2)
            dve.tensor_scalar(head_shift[:, :], head_rows[:, :], shift_rows[:, 0:1], None, ALU.mult
                              ).then_inc(const_dve, 1)
            dve.wait_ge(const_dve, 3)
            for j in range(GROUPS):
                ins = dve.tensor_copy(k_diag[96:P, j, :, :],
                                      head_shift[96:P, :].unsqueeze(2).broadcast_to([32, 4, TOK]))
            ins.then_inc(const_dve, 1)
            dve.wait_ge(set_done, 1)

            def step(mid_job, front_job, end_job, next_job, s):
                on_ticks(front, middle_tick, end_tick, mid_job, front_job, end_job, s,
                         split_expert if s == -1 else None)

            run_steps(dve, step)

        @block.gpsimd
        def _(pool):
            def front(job, piece, *at):
                if piece in ("long_stats", "stats", "hidden_stats"):
                    n = norm_no(job, {"long_stats": "long", "stats": "norm", "hidden_stats": "hidden"}[piece])
                    norm_var.wait(pool, job, n + 1)
                    pool.tensor_tensor(rstd[:, :], var_eps[:, :], power[:, :], ALU.pow
                                       ).then_inc(norm_rstd.handle, 1)
                elif piece == "long_scores":
                    b, = at
                    wait_emptied(pool, job, ("long_scores", b))
                    pairs = long_e[:, b, :, :].rearrange("p k (n r) -> p (k n) r", r=RATE)
                    pool.tensor_tensor(pairs, pairs,
                                       phase_of[:, :].unsqueeze(1).broadcast_to([P, 2 * S // RATE, RATE]), ALU.mult
                                       ).then_inc(long_masked.handle, 1)
                elif piece == "spread":
                    ring_full.wait(pool, job, 0)
                    parts_in.wait(pool, job, 16 * 24, apart=True)
                    for i in range(4):
                        ins = pool.tensor_scalar(k_diag[0:96, :, i, :], k4_groups[0:96, :, :],
                                                 head_rows[0:96, i:i + 1], 0.0, ALU.mult, ALU.add)
                    ins.then_inc(k_diag_ready.handle, 1)
                elif piece == "head":
                    k, = at
                    wait_emptied(pool, job, ("head", k), apart=True)
                    both = probs[:, k % 4, 0:2 * P].rearrange("p (a q) -> p a q", a=2)
                    pool.affine_select(out=both, in_=both, compare_op=ALU.is_ge, fill=0.0, base=0,
                                       pattern=[[0, 2], [1, P]], channel_multiplier=-1
                                       ).then_inc(probs_ready.handle, 1)

            def middle_tick(job, t):
                if t >= LAG and (t - LAG) % FC == FC - 1:
                    e = (t - LAG) // FC
                    y_free.wait(pool, job, e + 2)
                    added.wait(pool, job, e)
                    pool.tensor_tensor(acc[:, job.parity, :], acc[:, job.parity, :], gated[:, e % 2, :], ALU.add
                                       ).then_inc(added.handle, 1)

            def end_tick(job, t):
                if t == 2:
                    end_var_in.wait(pool, job, 1)
                    pool.tensor_tensor(end_rstd[:, :], end_var[:, :], power[:, :], ALU.pow
                                       ).then_inc(end_rstd_in.handle, 1)
                if t == 4:
                    end_normed.wait(pool, job, 1)
                    pool.tensor_tensor(end_norm[:, :, :], end_norm[:, :, :],
                                       g2_half[:, :].unsqueeze(1).broadcast_to([P, TT, D]), ALU.mult
                                       ).then_inc(end_scaled.handle, 1)

            pool.memset(ident[:, :], 0.0)
            pool.memset(causal[:, :, :], 0.0).then_inc(const_pool, 1)
            pool.wait_ge(const_pool, 1)
            pool.affine_select(out=ident[:, :], in_=ident[:, :], compare_op=ALU.not_equal, fill=1.0, base=0,
                               pattern=[[-1, P]], channel_multiplier=1).then_inc(const_pool, 1)
            pool.affine_select(out=causal[:, :, :], in_=causal[:, :, :], compare_op=ALU.is_ge, fill=MASKED, base=0,
                               pattern=[[0, 4], [-1, P]], channel_multiplier=1).then_inc(const_pool, 1)
            pool.wait_ge(const_dve, CONSTANTS)

            def step(mid_job, front_job, end_job, next_job, s):
                on_ticks(front, middle_tick, end_tick, mid_job, front_job, end_job, s)

            run_steps(pool, step)


_INS = ['L0_attn_x', 'L0_ffn_w_qkv', 'L0_ffn_w_o', 'L0_ffn_g1', 'L0_ffn_b1', 'L0_ffn_wg', 'L0_ffn_w1',
        'L0_ffn_bb1', 'L0_ffn_w2', 'L0_ffn_bb2', 'L0_ffn_g2', 'L0_ffn_b2']


def kernel(**inputs):
    import numpy as _np
    import concourse.bacc as _bacc
    from concourse import mybir as _mybir
    from concourse.bass_utils import run_bass_kernel_spmd as _run

    nc = _bacc.Bacc("TRN2", target_bir_lowering=False, num_devices=1)
    arrays, args = {}, []
    for name in _INS:
        a = _np.ascontiguousarray(inputs[name])
        arrays[f"in_{name}"] = a
        args.append(nc.dram_tensor(f"in_{name}", a.shape, _mybir.dt.from_np(a.dtype), kind="ExternalInput").ap())
    out = nc.dram_tensor("out_rows", [SEQS, S, D], _mybir.dt.float32, kind="ExternalOutput").ap()
    build(nc, *args, out)
    r = _run(nc, [arrays], core_ids=[0])
    return r.results[0]["out_rows"]
```

```python
from contextlib import ExitStack

import concourse.bass as bass
from concourse import mybir

ALU = mybir.AluOpType
ACT = mybir.ActivationFunctionType
AX = mybir.AxisListType
F32 = mybir.dt.float32
F32R = mybir.dt.float32r
BF16 = mybir.dt.bfloat16
U32 = mybir.dt.uint32

P = 128
SEQS, S, D = 16, 256, 128
HEADS, HD = 16, 8
E, F = 8, 512
RATE = 4
CHUNKS = SEQS // 2
TOK = 2 * S
TT = TOK // P
FC = F // P
HID = E * FC
GROUPS = 4
EPS = 1e-5
MASKED = -1e30
SLOT = 32

RING = 3
HIDDEN_BANKS = 3
LAG = 3
VLAG = 3
TICKS = HID + LAG


def score_parts(b, first, last):
    return [("scores", b, n // 3, n % 3) for n in range(first, last)]


def heads(b, scores=()):
    found, scores = [], list(scores)
    for n in range(HEADS):
        found.append(("head", HEADS * b + n))
        if n % 4 < 3 and scores:
            found.append(scores.pop(0))
    return found + scores


FRONT = {
    4: [("mask", 0)],
    6: [("mask", 1)],
    7: score_parts(0, 0, 2),
    8: [("residual",)] + score_parts(0, 2, 4),
    9: score_parts(0, 4, 6),
    10: score_parts(0, 6, 8),
    11: score_parts(0, 8, 10),
    12: score_parts(0, 10, 12),
    13: [("shift_columns", 0)] + score_parts(1, 0, 2),
    14: score_parts(1, 2, 4),
    15: [("shift", 0)] + heads(0, score_parts(1, 4, 12)) + [("shift_columns", 1), ("shift", 1)],
    16: [("last_values", 0)],
    18: [("rows", 0, 0), ("rows", 0, 1)],
    20: heads(1),
    21: [("last_values", 1)],
    23: [("rows", 1, 0), ("rows", 1, 1)],
    25: [("merge",), ("attn_out", 0), ("attn_out", 1)],
    26: [("hidden_stats",)],
    28: [("hidden_norm",)],
    30: [("hidden",)],
    31: [("split_hidden",)],
    32: [("route",)],
    33: [("gate_exp",)],
    34: [("gate",)],
}
LONG = {
    10: [("long_stats",)],
    11: [("long_norm",)],
    13: [("long_turn", 0), ("long_turn", 1)],
    15: [("long_scores", 0), ("long_scores", 1)],
    17: [("long_values", 0), ("long_values", 1)],
}
EARLY = {
    24: [("stats",)],
    28: [("norm",)],
    32: [("turn", 0), ("turn", 1)],
    33: [("queries_keys", 1), ("queries_keys", 0), ("project_values",)],
}
HIGH_BY_SCALAR = list(range(9, 15))
AHEAD_AT = (1, 10)
AHEAD = [t + n for t in FRONT if ("head", 0) in FRONT[t] or ("head", HEADS) in FRONT[t] for n in (1, 2)]
IN_RING = ("turn", "queries_keys", "project_values", "scores", "shift", "head", "rows", "merge", "attn_out",
           "hidden", "route", "long_turn", "long_scores", "long_values")


def pieces(with_long, tick=None):
    ticks = range(TICKS) if tick is None else [tick]
    return [p for t in ticks for p in (LONG.get(t, []) if with_long else []) + FRONT.get(t, [])]


def ring_uses(with_long, first):
    uses = [p for t in EARLY for p in EARLY[t] if p[0] in IN_RING]
    uses += [p for p in pieces(with_long) if p[0] in IN_RING]
    return {use: n + first for n, use in enumerate(uses)}


FRONT_USES = len(ring_uses(False, 0))
LONG_USES = len(ring_uses(True, 0)) - FRONT_USES
RING_USES = {(kind, with_long): ring_uses(with_long, LONG_USES if kind == "B" else 0)
             for kind in "AB" for with_long in (False, True)}
assert FRONT_USES % RING == LONG_USES % RING == 0


class LoopCount:

    def __init__(self, eng, c, few, begun):
        self.eng, self.c, self.few, self.begun = eng, c, few, begun
        self.multiples = {}
        self.sum = eng.alloc_register("count")

    def wait_ge(self, handle, factor, more, apart):
        if self.few and more:
            self.eng.reg_mul(self.sum, self.c, factor)
            self.eng.reg_add(self.sum, self.sum, more)
        elif self.few:
            self.eng.reg_mul(self.sum, self.c, factor - 1)
            self.eng.reg_add(self.sum, self.sum, self.c)
        else:
            if factor not in self.multiples:
                self.multiples[factor] = self.eng.alloc_register(f"count_by_{factor}")
                self.eng.reg_mul(self.multiples[factor], self.c, factor)
            if more:
                self.eng.reg_add(self.sum, self.multiples[factor], more)
            else:
                self.eng.reg_mul(self.sum, self.c, factor)
        if apart:
            self.eng.wait_ge(self.begun, 1)
        self.eng.wait_ge(handle, self.sum)


class Job:

    def __init__(self, kind, chunk, a, b, parity, before=None, loop=None):
        self.kind, self.chunk, self.a, self.b, self.parity = kind, chunk, a, b, parity
        self.before, self.loop = before, loop
        self.long = None
        if kind == "B" and before:
            before.long = self


def job_at(n):
    order = [("A", 0), ("A", 1)]
    for c in range(CHUNKS - 2):
        order += [("A", c + 2), ("B", c)]
    order += [("B", CHUNKS - 2), ("B", CHUNKS - 1)]
    if not 0 <= n < len(order):
        return None
    kind, chunk = order[n]
    return Job(kind, chunk, sum(k == "A" for k, _ in order[:n]), sum(k == "B" for k, _ in order[:n]), n % 2,
               job_at(n - 1))


JOBS = 2 * CHUNKS
TURNS = (JOBS - 8) // 2


def loop_jobs(loop):
    jobs = []
    for kind, n, a, b in (("A", 1, 1, -1), ("B", -1, 2, -1), ("A", 2, 2, 0), ("B", 0, 3, 0), ("A", 3, 3, 1)):
        jobs.append(Job(kind, loop.c + n, a, b, "AB".index(kind), jobs[-1] if jobs else None, loop))
    return jobs


class Signal:

    def __init__(self, handle, per_a, per_b=None):
        self.handle, self.per_a = handle, per_a
        self.per_b = per_a if per_b is None else per_b

    def value(self, job, count):
        return job.a * self.per_a + job.b * self.per_b + count

    def wait_ge(self, eng, job, count, apart=False):
        if job is None:
            return
        v = self.value(job, count)
        if job.loop:
            job.loop.wait_ge(self.handle, self.per_a + self.per_b, v, apart)
        elif v > 0:
            eng.wait_ge(self.handle, v)


def build(nc, x, w_qkv, w_o, g1, b1, wg, w1, bb1, w2, bb2, g2, b2, out):
    x_tiles = x.rearrange("(c q) (h p) d -> c p (q h) d", q=2, p=P)
    out_tiles = out.rearrange("(c q) (h p) d -> c p (q h) d", q=2, p=P)
    middle = nc.dram_tensor("after_first_ffn", [CHUNKS, P, TT, D], F32, kind="Internal").ap()
    parts = nc.dram_tensor("query_key_parts", [4, P, TOK], F32, kind="Internal").ap()

    with ExitStack() as ctx:
        def sb(name, shape, dt=F32):
            return ctx.enter_context(nc.sbuf_tensor(name, shape, dt))

        def sem(name):
            return ctx.enter_context(nc.semaphore(name))

        def signal(name, per_a, per_b=None):
            return Signal(sem(name), per_a, per_b)

        wqkv = sb("wqkv", [P, 3 * D])
        wo = sb("wo", [P, D])
        wgate = sb("wgate", [P, E])
        w1_hi, w1_lo = sb("w1_hi", [P, E, F], F32R), sb("w1_lo", [P, E, F], F32R)
        w2_hi, w2_lo = sb("w2_hi", [P, E, FC, D], F32R), sb("w2_lo", [P, E, FC, D], F32R)
        bb1_t = sb("bb1_t", [P, HID])
        bb2_twice = sb("bb2_twice", [2 * E, D])
        g1_col, b1_col = sb("g1_col", [P, 1]), sb("b1_col", [P, 1])
        g2_half, b2_half = sb("g2_half", [P, D]), sb("b2_half", [P, D])
        ident = sb("ident", [P, P])
        ident_bf = sb("ident_bf", [P, P], BF16)
        causal = sb("causal", [P, P], BF16)
        head_rows = sb("head_rows", [P, GROUPS])
        expert_no = sb("expert_no", [P, E])
        power = sb("power", [P, TT])
        phase_of = sb("phase_of", [P, RATE])
        shift_rows = sb("shift_rows", [P, 1])
        head_shift = sb("head_shift", [P, GROUPS])
        expert_rows = sb("expert_rows", [2 * E, E], F32R)

        x_first, x_second = sb("x_first", [P, TT, D]), sb("x_second", [P, TT, D])
        xn = sb("xn", [P, TT, D])
        xn_t = sb("xn_t", [P, TOK])
        qk = sb("qk", [P, 4, TOK], F32R)
        q4 = sb("q4", [P, GROUPS, TOK], F32R)
        k4 = sb("k4", [P, GROUPS * TOK])
        k_diag = sb("k_diag", [P, GROUPS, 4, TOK], F32R)
        values = sb("values", [P, TT, HEADS, SLOT])
        row_max = sb("row_max", [P, TT, HEADS])
        shift_hi = sb("shift_hi", [P, TT, HEADS], F32R)
        shift_cols = sb("shift_cols", [P, TT, GROUPS, 4, 8])
        attn_t = sb("attn_t", [P, GROUPS, S])
        denom = sb("denom", [P, TT, HEADS])
        stats = sb("stats", [P, 2, TT, 6])
        moments = sb("moments", [P, 2, TT, 2])
        var_eps, rstd = sb("var_eps", [P, 2, TT]), sb("rstd", [P, 2, TT])
        logits = sb("logits", [P, TT, E])
        top8, top8_at = sb("top8", [P, TT, 8]), sb("top8_at", [P, TT, 8], U32)
        top_at = sb("top_at", [P, 2, TT])
        gap, gap_exp = sb("gap", [P, TT]), sb("gap_exp", [P, TT])
        gate_den = sb("gate_den", [P, TT])
        gates = sb("gates", [P, 2, TT])
        chosen = sb("chosen", [P, 2 * TT, E])
        gate_w = sb("gate_w", [P, TT, E])
        gate_hi = sb("gate_hi", [P, TT, E], F32R)
        gate_parts = sb("gate_parts", [P, TT, 2 * E])

        k4_groups = k4[:, :].rearrange("p (j t) -> p j t", j=GROUPS)

        long_xn = sb("long_xn", [P, TT, 132])
        long_xn_t = sb("long_xn_t", [P, TOK])
        long_e = sb("long_e", [P, 2, 2, S])
        long_stats, long_moments = sb("long_stats", [P, TT, 6]), sb("long_moments", [P, TT, 2])
        long_var, long_rstd = sb("long_var", [P, TT]), sb("long_rstd", [P, TT])
        long_rec = sb("long_rec", [P, TT])

        probs = k4[:, 0:4 * 3 * P].rearrange("p (n c) -> p n c", n=4)
        attn_feat = xn_t
        attn = mid = long_xn_t[:, :].rearrange("p (t d) -> p t d", t=TT)

        acc = sb("acc", [P, 2, TOK])
        h_hi, h_lo = sb("h_hi", [P, 2, TOK], F32R), sb("h_lo", [P, 2, TOK], F32R)
        gate_rows = sb("gate_rows", [2 * E, 2, TOK], F32R)
        x_plus = sb("x_plus", [P, 2, TT, D])

        act = sb("act", [P, 2, TOK])
        act_hi, act_lo = sb("act_hi", [P, 4, TOK], F32R), sb("act_lo", [P, 4, TOK], F32R)
        gate_bc = sb("gate_bc", [P, 2, TOK])
        gated = sb("gated", [P, 2, TOK])
        rows, ones_row = gated[0:1, 0, 0:2 * D].rearrange("p (n d) -> p n d", n=2), gated[0:1, 1, 0:P]
        end_rows = sb("end_rows", [P, TT, D])
        end_stats, end_moments = sb("end_stats", [P, TT, 6]), sb("end_moments", [P, TT, 2])
        end_var, end_rstd = sb("end_var", [P, TT]), sb("end_rstd", [P, TT])

        ps_hidden = ctx.enter_context(nc.psum_tensor("ps_hidden", [P, HIDDEN_BANKS, 512], F32))
        ps_y = ctx.enter_context(nc.psum_tensor("ps_y", [P, 512], F32))
        ps_ring = ctx.enter_context(nc.psum_tensor("ps_ring", [P, RING, 512], F32))
        ps_attn = ctx.enter_context(nc.psum_tensor("ps_attn", [P, 512], F32))

        small_in = sem("small_in")
        weights_in = [sem(f"weights_in{i}") for i in range(2)]
        weights_hi, weights_lo = sem("weights_hi"), sem("weights_lo")
        const_dve, const_pool, const_mid = sem("const_dve"), sem("const_pool"), sem("const_mid")
        set_full, set_done = sem("set_full"), sem("set_done")

        x_first_in, x_second_in = signal("x_first_in", 16, 0), signal("x_second_in", 0, 16)
        norm_stats, norm_moments, norm_var, norm_rstd = [
            [signal(f"{which}_{what}", 1) for which in ("norm", "hidden")]
            for what in ("stats_in", "moments_in", "var_in", "rstd_in")]
        xn_ready, rows_used = signal("xn_ready", 1), signal("rows_used", 1)
        ring_full = signal("ring_full", FRONT_USES, FRONT_USES + LONG_USES)
        ring_free = [signal(f"ring_free{i}", FRONT_USES // RING, (FRONT_USES + LONG_USES) // RING)
                     for i in range(RING)]
        attn_free = signal("attn_free", 4)
        qk_hi = signal("qk_hi", 2)
        keys_out, queries_out = signal("keys_out", 16), signal("queries_out", 16)
        keys_in, queries_in = signal("keys_in", 16 * 3), signal("queries_in", 16 * 3)
        k_diag_first, k_diag_last = signal("k_diag_first", 2), signal("k_diag_last", 2)
        shift_hi_ready, shift_ready = signal("shift_hi_ready", 2), signal("shift_ready", 2)
        probs_ready, values_done = signal("probs_ready", 32), signal("values_done", 32)
        denom_ready = signal("denom_ready", 4)
        mid_ready = signal("mid_ready", 1)
        h_hi_ready, h_ready = signal("h_hi_ready", 1), signal("h_ready", 1)
        top_ready, top_at_ready, gap_ready = signal("top_ready", 1), signal("top_at_ready", 1), signal("gap_ready", 1)
        gap_exp_ready, chosen_ready = signal("gap_exp_ready", 1), signal("chosen_ready", 1)
        gate_step, gate_ready = signal("gate_step", 6), signal("gate_ready", 1)

        long_stats_in, long_moments_in = signal("long_stats_in", 0, 1), signal("long_moments_in", 0, 1)
        long_var_in, long_rstd_in = signal("long_var_in", 0, 1), signal("long_rstd_in", 0, 1)
        long_xn_ready, long_masked = signal("long_xn_ready", 0, 1), signal("long_masked", 0, 2)
        long_recip = signal("long_recip", 0, 2)

        hidden_full, hidden_free = signal("hidden_full", HID + E), signal("hidden_free", HID + E)
        act_hi_ready, act_ready = signal("act_hi_ready", HID - len(HIGH_BY_SCALAR)), signal("act_ready", HID)
        scalar_hi_ready = signal("scalar_hi_ready", len(HIGH_BY_SCALAR))
        act_used = signal("act_used", HID)
        gate_turned, gate_rows_ready = signal("gate_turned", 1), signal("gate_rows_ready", 1)
        bias_full, bias_used = signal("bias_full", 1), signal("bias_used", 1)
        y_free = signal("y_free", E + 1)
        added = signal("added", E)
        turned = signal("turned", 1)
        end_stats_in, end_moments_in = signal("end_stats_in", 1), signal("end_moments_in", 1)
        end_var_in, end_rstd_in = signal("end_var_in", 1), signal("end_rstd_in", 1)
        end_normed, end_scaled = signal("end_normed", 1), signal("end_scaled", 1)
        result_ready, stored = signal("result_ready", 1), signal("stored", 16)

        def ring_no(job, use):
            return RING_USES[job.kind, job.long is not None][use]

        def ring_bank(job, use):
            return ps_ring[:, ring_no(job, use) % RING, :]

        def bank_free(job, use):
            return ring_free[ring_no(job, use) % RING]

        def times_used(job, use):
            return ring_no(job, use) // RING

        def hidden_use(t):
            return t + t // FC

        def gates_use(e):
            return hidden_use(FC * e + FC - 1) + 1

        def norm_no(which):
            return ("norm", "hidden").index(which)

        def on_ticks(engine_front, engine_long, engine_middle, engine_end, jobs, s, setup=None, ahead=False, sums=None):
            middle, front, end, following = jobs
            if s == -1:
                for t in EARLY:
                    for piece in EARLY[t]:
                        engine_front(front, *piece)
            for t in range(TICKS):
                if middle and sums and not (front and t in AHEAD):
                    sums(middle, t)
                if middle and not (ahead and front and t in AHEAD):
                    engine_middle(middle, t)
                if end:
                    engine_end(end, t)
                if setup and t < E // 2:
                    setup(2 * t)
                    setup(2 * t + 1)
                if front:
                    for piece in pieces(front.long is not None, t):
                        if piece[0].startswith("long"):
                            engine_long(front.long, front, *piece)
                        else:
                            engine_front(front, *piece)
                        if ahead and middle and piece[0] == "head" and piece[1] % HEADS in AHEAD_AT:
                            engine_middle(middle, t + 1 + AHEAD_AT.index(piece[1] % HEADS))
                if middle and sums and front and t + 1 in AHEAD and t not in AHEAD:
                    sums(middle, t + 1)
                    sums(middle, t + 2)
                if following:
                    for piece in EARLY.get(t, []):
                        engine_front(following, *piece)

        def run_steps(eng, one_step):
            def step(middle, front, end, following, s=None):
                for job, after in ((middle, front), (front, following)):
                    if job and after and after.kind == "B":
                        job.long = after
                one_step((middle, front, end, following), s)

            for s in range(-1, 3):
                step(job_at(s), job_at(s + 1), job_at(s - 1), job_at(s + 2), s)
            with eng.Fori(1, TURNS + 1) as c:
                jobs = loop_jobs(LoopCount(eng, c, eng is nc.sync, const_dve))
                step(jobs[1], jobs[2], jobs[0], jobs[3])
                step(jobs[2], jobs[3], jobs[1], jobs[4])
            for s in range(2 * TURNS + 3, JOBS + 1):
                step(job_at(s), job_at(s + 1), job_at(s - 1), job_at(s + 2), s)

        stage = [k4[:, 0:2 * F], k4[:, 2 * F:4 * F]]
        bb1_rows = end_rows[0:HID, 0, :]

        CONSTANTS = 4

        block = ctx.enter_context(nc.Block())

        @block.sync
        def _(sp):
            def load(job, front, end=None):
                rows_used.wait_ge(sp, front, 1 if job.kind == front.kind and job is not front else 0)
                if job.kind == "B":
                    if job.loop:
                        stored.wait_ge(sp, end, 0)
                    else:
                        stored.wait_ge(sp, Job("A", job.chunk, job.chunk, max(job.chunk - 2, 0), 0), 16)
                    sp.dma_start(x_second[:, :, :], middle[job.chunk]).then_inc(x_second_in.handle, 16)
                else:
                    sp.dma_start(x_first[:, :, :], x_tiles[job.chunk]).then_inc(x_first_in.handle, 16)

            def spread(job):
                keys_in.wait_ge(sp, job, 0)
                queries_in.wait_ge(sp, job, 0)
                for which, out_of, first in ((1, keys_out, 2), (0, queries_out, 0)):
                    use = ("queries_keys", which)
                    bank_free(job, use).wait_ge(sp, job, times_used(job, use) + 1)
                    sp.dma_start(parts[first:first + 2].rearrange("n p t -> p n t"),
                                 qk[:, first:first + 2, :].bitcast(F32)).then_inc(out_of.handle, 16)
                values_done.wait_ge(sp, job, 0)
                k_diag_first.wait_ge(sp, job, 0)
                k_diag_last.wait_ge(sp, job, 0)
                if job.kind == "A" and isinstance(job.chunk, int) and job.chunk == 0:
                    sp.wait_ge(weights_lo, E)
                for to, out_of, into, of in ((k4_groups, keys_out, keys_in, (2, 3, 2)),
                                             (q4[:, :, :].bitcast(F32), queries_out, queries_in, (0, 0, 1))):
                    out_of.wait_ge(sp, job, 16)
                    for row, part in enumerate(of):
                        sp.dma_start(to[32 * row:32 * row + 32, :, :],
                                     parts[part].rearrange("(j p) t -> p j t", j=GROUPS)
                                     ).then_inc(into.handle, 16)

            def store(job):
                result_ready.wait_ge(sp, job, 1)
                target = middle if job.kind == "A" else out_tiles
                sp.dma_start(target[job.chunk], end_rows[:, :, :]).then_inc(stored.handle, 16)

            def load_expert(e):
                if e >= 2:
                    sp.wait_ge(weights_hi, e - 1)
                    sp.wait_ge(weights_lo, e - 1)
                sp.dma_start(stage[e % 2][:, 0:F], w1[e]).then_inc(weights_in[e % 2], 16)
                sp.dma_start(stage[e % 2][:, F:2 * F].rearrange("p (c n) -> p c n", c=FC),
                             w2[e].rearrange("(c p) n -> p c n", p=P)).then_inc(weights_in[e % 2], 16)

            sp.dma_start(wqkv[:, :], w_qkv).then_inc(small_in, 16)
            sp.dma_start(wo[:, :], w_o).then_inc(small_in, 16)
            sp.dma_start(wgate[:, :], wg).then_inc(small_in, 16)
            sp.dma_start(g1_col[:, :], g1.rearrange("(p a) -> p a", a=1)).then_inc(small_in, 16)
            sp.dma_start(b1_col[:, :], b1.rearrange("(p a) -> p a", a=1)).then_inc(small_in, 16)
            sp.dma_start(rows[:, 0, :], g2.rearrange("(a n) -> a n", a=1)).then_inc(small_in, 16)
            sp.dma_start(rows[:, 1, :], b2.rearrange("(a n) -> a n", a=1)).then_inc(small_in, 16)
            sp.dma_start(bb2_twice[0:E, :], bb2).then_inc(small_in, 16)
            sp.dma_start(bb2_twice[E:2 * E, :], bb2).then_inc(small_in, 16)
            sp.dma_start(bb1_rows, bb1.rearrange("e (c p) -> (e c) p", p=P)).then_inc(small_in, 16)

            def step(jobs, s):
                _, front, end, following = jobs
                if s == -1:
                    load(front, front)
                    for e in range(E):
                        load_expert(e)
                    spread(front)
                early = front and following and (front.kind, following.kind) == ("B", "A")
                if early:
                    load(following, front, end)
                if end:
                    store(end)
                if following and not early:
                    load(following, front, end)
                if following:
                    spread(following)

            run_steps(sp, step)
            stored.wait_ge(sp, Job("B", 0, CHUNKS, CHUNKS, 0), 0)

        @block.tensor
        def _(pe):
            def front(job, piece, *at):
                use = (piece,) + at
                if piece == "turn":
                    xn_ready.wait_ge(pe, job, 1)
                    bank_free(job, use).wait_ge(pe, job, times_used(job, use))
                    for n in range(2):
                        mm = pe.transpose(ring_bank(job, use)[:, n * P:(n + 1) * P], xn[:, 2 * at[0] + n, :],
                                          ident[:, :])
                    mm.then_inc(ring_full.handle, 1)
                elif piece == "queries_keys":
                    which, = at
                    bank_free(job, ("turn", 0)).wait_ge(pe, job, times_used(job, ("turn", 0)) + 1)
                    bank_free(job, ("turn", 1)).wait_ge(pe, job, times_used(job, ("turn", 1)) + 1)
                    bank_free(job, use).wait_ge(pe, job, times_used(job, use))
                    pe.matmul(ring_bank(job, use), wqkv[:, which * D:(which + 1) * D], xn_t[:, :],
                              start=True, stop=True).then_inc(ring_full.handle, 1)
                elif piece == "project_values":
                    bank_free(job, use).wait_ge(pe, job, times_used(job, use))
                    for tt in range(TT):
                        mm = pe.matmul(ring_bank(job, use)[:, tt * P:(tt + 1) * P], xn_t[:, tt * P:(tt + 1) * P],
                                       wqkv[:, 2 * D:3 * D], start=True, stop=True)
                    mm.then_inc(ring_full.handle, 1)
                elif piece == "scores":
                    b, j, part = at
                    if at == (0, 0, 0):
                        queries_in.wait_ge(pe, job, 16 * 3)
                    if (j, part) == (0, 0):
                        k_diag_first.wait_ge(pe, job, b + 1)
                        k_diag_last.wait_ge(pe, job, b + 1)
                    bank_free(job, use).wait_ge(pe, job, times_used(job, use))
                    bank = ring_bank(job, use)
                    if part == 0:
                        pe.matmul(bank, q4[0:96, j, b * S:b * S + P],
                                  k_diag[0:96, j, :, b * S:b * S + P], start=True, stop=False)
                        mm = pe.matmul(bank, ident_bf[:, :], causal[:, :].unsqueeze(1).broadcast_to([P, 4, P]),
                                       start=False, stop=True)
                    else:
                        i = 2 * (part - 1)
                        pe.matmul(bank, q4[0:96, j, b * S + P:(b + 1) * S],
                                  k_diag[0:96, j, i:i + 2, b * S:(b + 1) * S], start=True, stop=False)
                        mm = pe.matmul(bank.rearrange("p (i k) -> p i k", i=2)[:, :, P:S], ident_bf[:, :],
                                       causal[:, :].unsqueeze(1).broadcast_to([P, 2, P]), start=False, stop=True)
                    mm.then_inc(ring_full.handle, 1)
                elif piece == "shift":
                    b, = at
                    shift_ready.wait_ge(pe, job, b + 1)
                    bank_free(job, use).wait_ge(pe, job, times_used(job, use))
                    for n in range(2):
                        mm = pe.transpose(ring_bank(job, use)[:, n * P:(n + 1) * P],
                                          shift_cols[:, 2 * b + n, :, :, :].rearrange("p j i c -> p (j i c)"),
                                          ident[:, :])
                    mm.then_inc(ring_full.handle, 1)
                elif piece == "head":
                    k, = at
                    b, j, i = k // HEADS, k % HEADS // 4, k % 4
                    if k % HEADS == 0:
                        bank_free(job, ("shift", b)).wait_ge(pe, job, times_used(job, ("shift", b)) + 1)
                    bank_free(job, use).wait_ge(pe, job, times_used(job, use))
                    bank = ring_bank(job, use)
                    pe.matmul(bank[:, 0:S], k_diag[:, j, i, b * S + P:(b + 1) * S],
                              q4[:, j, b * S:(b + 1) * S], start=True, stop=True)
                    pe.matmul(bank[:, S:2 * S], k_diag[:, j, i, b * S:b * S + P],
                              q4[:, j, b * S:(b + 1) * S], start=True, stop=True
                              ).then_inc(ring_full.handle, 1)
                    if k % HEADS >= VLAG:
                        head_values(job, k - VLAG)
                    if k % HEADS == HEADS - 1:
                        for late in range(k - VLAG + 1, k + 1):
                            head_values(job, late)
                elif piece == "rows":
                    b, qt = at
                    attn_free.wait_ge(pe, job, 2 * b + 2)
                    bank_free(job, use).wait_ge(pe, job, times_used(job, use))
                    for j in range(GROUPS):
                        mm = pe.transpose(ring_bank(job, use)[:, j * P:(j + 1) * P],
                                          attn_t[:, j, qt * P:(qt + 1) * P], ident[:, :])
                    mm.then_inc(ring_full.handle, 1)
                elif piece == "merge":
                    for b in range(2):
                        for qt in range(2):
                            bank_free(job, ("rows", b, qt)).wait_ge(pe, job, times_used(job, ("rows", b, qt)) + 1)
                    bank_free(job, use).wait_ge(pe, job, times_used(job, use))
                    for tt in range(TT):
                        mm = pe.transpose(ring_bank(job, use)[:, tt * P:(tt + 1) * P], attn[:, tt, :], ident[:, :])
                    mm.then_inc(ring_full.handle, 1)
                elif piece == "attn_out":
                    half, = at
                    bank_free(job, ("merge",)).wait_ge(pe, job, times_used(job, ("merge",)) + 1)
                    bank_free(job, use).wait_ge(pe, job, times_used(job, use))
                    for n in range(2):
                        tt = 2 * half + n
                        mm = pe.matmul(ring_bank(job, use)[:, n * P:(n + 1) * P],
                                       attn_feat[:, tt * P:(tt + 1) * P], wo[:, :], start=True, stop=True)
                    mm.then_inc(ring_full.handle, 1)
                elif piece == "hidden":
                    mid_ready.wait_ge(pe, job, 1)
                    bank_free(job, use).wait_ge(pe, job, times_used(job, use))
                    for tt in range(TT):
                        mm = pe.transpose(ring_bank(job, use)[:, tt * P:(tt + 1) * P], mid[:, tt, :], ident[:, :])
                    mm.then_inc(ring_full.handle, 1)
                elif piece == "route":
                    bank_free(job, ("hidden",)).wait_ge(pe, job, times_used(job, ("hidden",)) + 1)
                    bank_free(job, use).wait_ge(pe, job, times_used(job, use))
                    for tt in range(TT):
                        mm = pe.matmul(ring_bank(job, use)[:, tt * E:(tt + 1) * E],
                                       acc[:, job.parity, tt * P:(tt + 1) * P], wgate[:, :], start=True, stop=True)
                    mm.then_inc(ring_full.handle, 1)

            def long(job, host, piece, *at):
                use = (piece,) + at
                at = at[0] if at else None
                if piece == "long_turn":
                    long_xn_ready.wait_ge(pe, job, 1)
                    bank_free(host, use).wait_ge(pe, host, times_used(host, use))
                    for n in range(2):
                        mm = pe.transpose(ring_bank(host, use)[:, n * P:(n + 1) * P],
                                          long_xn[:, 2 * at + n, 0:D], ident[:, :])
                    mm.then_inc(ring_full.handle, 1)
                elif piece == "long_scores":
                    bank_free(host, ("long_turn", at)).wait_ge(pe, host, times_used(host, ("long_turn", at)) + 1)
                    bank_free(host, use).wait_ge(pe, host, times_used(host, use))
                    for kt in range(2):
                        mm = pe.matmul(ring_bank(host, use)[:, kt * S:(kt + 1) * S],
                                       long_xn_t[:, at * S + kt * P:at * S + (kt + 1) * P],
                                       long_xn_t[:, at * S:(at + 1) * S], start=True, stop=True)
                    mm.then_inc(ring_full.handle, 1)
                elif piece == "long_values":
                    long_masked.wait_ge(pe, job, at + 1)
                    bank_free(host, use).wait_ge(pe, host, times_used(host, use))
                    for qt in range(2):
                        for kt in range(2):
                            mm = pe.matmul(ring_bank(host, use)[:, qt * S:qt * S + D + 1],
                                           long_e[:, at, kt, qt * P:(qt + 1) * P], long_xn[:, 2 * at + kt, 0:D + 1],
                                           start=(kt == 0), stop=(kt == 1))
                    mm.then_inc(ring_full.handle, 1)

            def head_values(job, k):
                b, j, i = k // HEADS, k % HEADS // 4, k % 4
                if k == 0:
                    bank_free(job, ("project_values",)).wait_ge(pe, job, times_used(job, ("project_values",)) + 1)
                if k == 0:
                    bias_used.wait_ge(pe, job.before, 1)
                if k % 8 == 0:
                    attn_free.wait_ge(pe, job, k // 8)
                probs_ready.wait_ge(pe, job, k + 1)
                to = ps_attn[32 * i:32 * i + SLOT, (j % 2) * S:(j % 2 + 1) * S]
                pe.matmul(to, values[:, 2 * b, 4 * j + i, :], probs[:, k % 4, P:3 * P], start=True, stop=False,
                          tile_position=(0, 32 * i))
                pe.matmul(to[:, P:S], values[:, 2 * b + 1, 4 * j + i, :], probs[:, k % 4, 0:P], start=False,
                          stop=True, tile_position=(0, 32 * i)).then_inc(values_done.handle, 1)

            def middle_tick(job, t):
                if t < HID:
                    e, f = t // FC, t % FC
                    if t == 0:
                        h_ready.wait_ge(pe, job, 1)
                    n = hidden_use(t)
                    hidden_free.wait_ge(pe, job, max(n - HIDDEN_BANKS + 1, 0))
                    to, cols = ps_hidden[:, n % HIDDEN_BANKS, :], slice(f * P, (f + 1) * P)
                    pe.matmul(to, w1_hi[:, e, cols], h_hi[:, job.parity, :], start=True, stop=False)
                    pe.matmul(to, w1_hi[:, e, cols], h_lo[:, job.parity, :], start=False, stop=False)
                    pe.matmul(to, w1_lo[:, e, cols], h_hi[:, job.parity, :], start=False, stop=True
                              ).then_inc(hidden_full.handle, 1)
                    if f == FC - 1:
                        n = gates_use(e)
                        if e == 0:
                            gate_rows_ready.wait_ge(pe, job, 1)
                        hidden_free.wait_ge(pe, job, max(n - HIDDEN_BANKS + 1, 0))
                        pe.matmul(ps_hidden[:, n % HIDDEN_BANKS, :], expert_rows[:, e:e + 1].broadcast_to([2 * E, P]),
                                  gate_rows[:, job.parity, :],
                                  start=True, stop=True).then_inc(hidden_full.handle, 1)
                if t == 2:
                    gate_ready.wait_ge(pe, job, 1)
                    attn_free.wait_ge(pe, job, 4)
                    for tt in range(TT):
                        mm = pe.transpose(ps_attn[0:2 * E, tt * P:(tt + 1) * P], gate_parts[:, tt, :], ident[:, :])
                    mm.then_inc(gate_turned.handle, 1)
                if t == 3:
                    gate_rows_ready.wait_ge(pe, job, 1)
                    pe.matmul(ps_attn[:, :], bb2_twice[:, :], gate_rows[:, job.parity, :].bitcast(F32),
                              start=True, stop=True).then_inc(bias_full.handle, 1)
                if t >= LAG:
                    u = t - LAG
                    e, f = u // FC, u % FC
                    if f == 0:
                        y_free.wait_ge(pe, job, e)
                    act_ready.wait_ge(pe, job, u + 1)
                    pe.matmul(ps_y[:, :], w2_hi[:, e, f, :], act_hi[:, u % 4, :], start=(f == 0), stop=False)
                    pe.matmul(ps_y[:, :], w2_hi[:, e, f, :], act_lo[:, u % 4, :], start=False, stop=False)
                    pe.matmul(ps_y[:, :], w2_lo[:, e, f, :], act_hi[:, u % 4, :], start=False, stop=(f == FC - 1)
                              ).then_inc(act_used.handle, 1)

            def end_tick(job, t):
                if t == 2:
                    added.wait_ge(pe, job, E)
                    y_free.wait_ge(pe, job, E)
                    for tt in range(TT):
                        mm = pe.transpose(ps_y[:, tt * P:(tt + 1) * P], acc[:, job.parity, tt * P:(tt + 1) * P],
                                          ident[:, :])
                    mm.then_inc(turned.handle, 1)

            pe.wait_ge(small_in, 16 * 10)
            pe.wait_ge(const_pool, 3)
            pe.wait_ge(const_dve, CONSTANTS)
            pe.matmul(ps_attn[:, 0:2 * D], ones_row[:, :], rows[:, :, :], start=True, stop=True)
            pe.transpose(ps_attn[:, 2 * D:2 * D + HID], bb1_rows, ident[0:HID, 0:HID]).then_inc(set_full, 1)

            def step(jobs, s):
                if s == 0:
                    pe.wait_ge(weights_hi, E)
                    pe.wait_ge(weights_lo, E)
                if s == -1:
                    pe.wait_ge(set_done, 1)
                on_ticks(front, long, middle_tick, end_tick, jobs, s, ahead=True)

            run_steps(pe, step)

        @block.scalar
        def _(act_eng):
            sc = act_eng

            def front(job, piece, *at):
                use = (piece,) + at
                if piece == "turn":
                    ring_full.wait_ge(sc, job, ring_no(job, use) + 1)
                    sc.activation(xn_t[:, at[0] * S:(at[0] + 1) * S], ring_bank(job, use)[:, 0:S], ACT.Copy
                                  ).then_inc(bank_free(job, use).handle, 1)
                elif piece == "queries_keys":
                    (keys_out if at[0] else queries_out).wait_ge(sc, job, 0)
                    ring_full.wait_ge(sc, job, ring_no(job, use) + 1)
                    sc.activation(qk[:, 2 * at[0], :], ring_bank(job, use), ACT.Copy).then_inc(qk_hi.handle, 1)
                elif piece == "project_values":
                    ring_full.wait_ge(sc, job, ring_no(job, use) + 1)
                    sc.activation(values[:, :, :, 0:HD],
                                  ring_bank(job, use).rearrange("p (t h d) -> p t h d", t=TT, h=HEADS), ACT.Copy
                                  ).then_inc(bank_free(job, use).handle, 1)
                elif piece == "mask":
                    b, = at
                    if b == 0:
                        values_done.wait_ge(sc, job, 0)
                        keys_in.wait_ge(sc, job, 16 * 3)
                    cols = slice(b * S, (b + 1) * S)
                    for i in range(2, 4):
                        ins = sc.activation(k_diag[0:96, :, i, cols], k4_groups[0:96, :, cols], ACT.Copy,
                                            scale=head_rows[0:96, i:i + 1])
                    ins.then_inc(k_diag_last.handle, 1)
                elif piece == "shift":
                    b, = at
                    ring_full.wait_ge(sc, job, ring_no(job, use) + 1)
                    for j in range(GROUPS):
                        ins = sc.activation(q4[96:128, j, b * S:(b + 1) * S],
                                            ring_bank(job, use)[32 * j:32 * j + 32, 0:S], ACT.Copy)
                    ins.then_inc(bank_free(job, use).handle, 1)
                elif piece == "head":
                    k, = at
                    values_done.wait_ge(sc, job, k - 3)
                    if k == 0:
                        k_diag_first.wait_ge(sc, job, 2)
                    ring_full.wait_ge(sc, job, ring_no(job, use) + 1)
                    sc.activation(probs[:, k % 4, :], ring_bank(job, use)[:, P:4 * P], ACT.Exp, scale=HD ** -0.5
                                  ).then_inc(bank_free(job, use).handle, 1)
                    if k % HEADS == 7 + VLAG:
                        attn_copy(job, 2 * (k // HEADS))
                elif piece == "last_values":
                    attn_copy(job, 2 * at[0] + 1)
                elif piece == "merge":
                    ring_full.wait_ge(sc, job, ring_no(job, use) + 1)
                    sc.activation(attn_feat[:, :], ring_bank(job, use), ACT.Copy
                                  ).then_inc(bank_free(job, use).handle, 1)
                elif piece == "hidden":
                    turned.wait_ge(sc, job.before, 0)
                    ring_full.wait_ge(sc, job, ring_no(job, use) + 1)
                    sc.activation(acc[:, job.parity, :], ring_bank(job, use), ACT.Identity, bias=b1_col[:, 0:1],
                                  scale=g1_col[:, 0:1]).then_inc(bank_free(job, use).handle, 1)
                elif piece == "gate_exp":
                    gap_ready.wait_ge(sc, job, 1)
                    sc.activation(gap_exp[:, :], gap[:, :], ACT.Exp).then_inc(gap_exp_ready.handle, 1)

            def long(job, host, piece, *at):
                use = (piece,) + at
                if piece == "long_turn":
                    ring_full.wait_ge(sc, host, ring_no(host, use) + 1)
                    sc.activation(long_xn_t[:, at[0] * S:(at[0] + 1) * S], ring_bank(host, use)[:, 0:S], ACT.Copy
                                  ).then_inc(bank_free(host, use).handle, 1)
                elif piece == "long_scores":
                    ring_full.wait_ge(sc, host, ring_no(host, use) + 1)
                    sc.activation(long_e[:, at[0], :, :].rearrange("p k q -> p (k q)"), ring_bank(host, use),
                                  ACT.Exp, scale=D ** -0.5).then_inc(bank_free(host, use).handle, 1)

            def attn_copy(job, n):
                values_done.wait_ge(sc, job, 8 * n + 8)
                if n == 2:
                    ring_full.wait_ge(sc, job, ring_no(job, ("rows", 0, 1)) + 1)
                sc.activation(attn_t[:, 2 * (n % 2):2 * (n % 2) + 2, :].rearrange("p j q -> p (j q)"),
                              ps_attn[:, :], ACT.Copy).then_inc(attn_free.handle, 1)

            def middle_tick(job, t):
                if t >= HID:
                    return
                e, f = t // FC, t % FC
                if t == 2:
                    gate_turned.wait_ge(sc, job, 1)
                    sc.activation(gate_rows[:, job.parity, :], ps_attn[0:2 * E, :], ACT.Copy
                                  ).then_inc(gate_rows_ready.handle, 1)
                n = hidden_use(t)
                act_ready.wait_ge(sc, job, t - 1)
                hidden_full.wait_ge(sc, job, n + 1)
                if t in HIGH_BY_SCALAR:
                    act_used.wait_ge(sc, job, t - 3)
                    sc.activation(act_hi[:, t % 4, :], ps_hidden[:, n % HIDDEN_BANKS, :], ACT.Gelu_apprx_tanh,
                                  bias=bb1_t[:, t:t + 1]).then_inc(scalar_hi_ready.handle, 1)
                sc.activation(act[:, t % 2, :], ps_hidden[:, n % HIDDEN_BANKS, :], ACT.Gelu_apprx_tanh,
                              bias=bb1_t[:, t:t + 1]
                              ).then_inc(hidden_free.handle, 1)
                if f == FC - 1:
                    n = gates_use(e)
                    hidden_full.wait_ge(sc, job, n + 1)
                    if e >= 2:
                        y_free.wait_ge(sc, job, e - 1)
                    sc.activation(gate_bc[:, e % 2, :], ps_hidden[:, n % HIDDEN_BANKS, :], ACT.Copy
                                  ).then_inc(hidden_free.handle, 1)

            def end_tick(job, t):
                if t == 2:
                    turned.wait_ge(sc, job, 1)
                    stored.wait_ge(sc, job, 0)
                    sc.activation(end_rows[:, :, :].rearrange("p t d -> p (t d)"), ps_y[:, :], ACT.Copy
                                  ).then_inc(y_free.handle, 1)

            def split_expert(e):
                sc.wait_ge(weights_in[e % 2], 32 * (e // 2 + 1))
                sc.activation(w1_hi[:, e, :], stage[e % 2][:, 0:F], ACT.Copy)
                sc.activation(w2_hi[:, e, :, :].rearrange("p c n -> p (c n)"), stage[e % 2][:, F:2 * F], ACT.Copy
                              ).then_inc(weights_hi, 1)

            sc.wait_ge(set_full, 1)
            sc.activation(g2_half[:, :], ps_attn[:, 0:D], ACT.Copy, scale=0.5)
            sc.activation(b2_half[:, :], ps_attn[:, D:2 * D], ACT.Copy, scale=0.5)
            sc.activation(bb1_t[:, :], ps_attn[:, 2 * D:2 * D + HID], ACT.Copy).then_inc(set_done, 1)

            def step(jobs, s):
                if s == 0:
                    sc.wait_ge(weights_lo, E)
                on_ticks(front, long, middle_tick, end_tick, jobs, s,
                         split_expert if s == -1 else None)

            run_steps(sc, step)

        @block.vector
        def _(dve):
            def norm_statistics(job, which, rows_of):
                n = norm_no(which)
                for tt in range(TT):
                    ins = dve.bn_stats(stats[:, n, tt, :], rows_of(tt))
                ins.then_inc(norm_stats[n].handle, 1)
                norm_stats[n].wait_ge(dve, job, 1, apart=True)
                for tt in range(TT):
                    ins = dve.bn_aggr(moments[:, n, tt, :], stats[:, n, tt, :])
                ins.then_inc(norm_moments[n].handle, 1)
                norm_moments[n].wait_ge(dve, job, 1)
                dve.tensor_scalar(var_eps[:, n, :], moments[:, n, :, 1], EPS, None, ALU.add
                                  ).then_inc(norm_var[n].handle, 1)

            def normalise(job, which, to, rows_of):
                n = norm_no(which)
                norm_rstd[n].wait_ge(dve, job, 1)
                for tt in range(TT):
                    ins = dve.tensor_scalar(to(tt), rows_of(tt), moments[:, n, tt, 0:1], rstd[:, n, tt:tt + 1],
                                            ALU.subtract, ALU.mult)
                return ins

            def front(job, piece, *at):
                use = (piece,) + at
                rows_in = x_first if job.kind == "A" else x_second
                if piece == "stats":
                    if job.kind == "A":
                        x_first_in.wait_ge(dve, job, 16)
                    else:
                        for b in range(2):
                            use = ("long_values", b)
                            bank_free(job.before, use).wait_ge(dve, job.before, times_used(job.before, use) + 1)
                    norm_statistics(job, "norm", lambda tt: rows_in[:, tt, :])
                elif piece == "norm":
                    normalise(job, "norm", lambda tt: xn[:, tt, :], lambda tt: rows_in[:, tt, :]
                              ).then_inc(xn_ready.handle, 1)
                elif piece == "queries_keys":
                    which, = at
                    qk_hi.wait_ge(dve, job, 2 - which)
                    dve.tensor_tensor(qk[:, 2 * which + 1, :], ring_bank(job, use), qk[:, 2 * which, :].bitcast(F32),
                                      ALU.subtract).then_inc(bank_free(job, use).handle, 1)
                elif piece == "scores":
                    b, j, part = at
                    ring_full.wait_ge(dve, job, ring_no(job, use) + 1)
                    if part == 0:
                        to, n = row_max[:, 2 * b, 4 * j:4 * j + 4], 4
                    else:
                        i = 4 * j + 2 * (part - 1)
                        to, n = row_max[:, 2 * b + 1, i:i + 2], 2
                    dve.tensor_reduce(to, ring_bank(job, use).rearrange("p (i k) -> p i k", i=n), AX.X, ALU.max
                                      ).then_inc(bank_free(job, use).handle, 1)
                elif piece == "shift_columns":
                    b, = at
                    last = ("scores", b, GROUPS - 1, 2)
                    bank_free(job, last).wait_ge(dve, job, times_used(job, last) + 1)
                    high, low = shift_hi[:, 2 * b:2 * b + 2, :], row_max[:, 2 * b:2 * b + 2, :]
                    dve.tensor_scalar(high, low, -1.0, None, ALU.mult).then_inc(shift_hi_ready.handle, 1)
                    shift_hi_ready.wait_ge(dve, job, b + 1)
                    cols = shift_cols[:, 2 * b:2 * b + 2, :, :, :].rearrange("p t j i c -> p t (j i) c")
                    dve.tensor_copy(cols[:, :, :, 0], high.bitcast(F32))
                    dve.scalar_tensor_tensor(out=cols[:, :, :, 1], in0=low, scalar=-1.0, in1=high.bitcast(F32),
                                             op0=ALU.mult, op1=ALU.subtract).then_inc(shift_ready.handle, 1)
                elif piece == "rows":
                    b, qt = at
                    tt = 2 * b + qt
                    ring_full.wait_ge(dve, job, ring_no(job, use) + 1)
                    heads = ring_bank(job, use).rearrange("p (h c) -> p h c", h=HEADS)
                    dve.reciprocal(denom[:, tt, :], heads[:, :, HD]).then_inc(denom_ready.handle, 1)
                    denom_ready.wait_ge(dve, job, tt + 1)
                    dve.tensor_tensor(attn[:, tt, :].rearrange("p (h d) -> p h d", h=HEADS), heads[:, :, 0:HD],
                                      denom[:, tt, :].unsqueeze(2).broadcast_to([P, HEADS, HD]), ALU.mult
                                      ).then_inc(bank_free(job, use).handle, 1)
                elif piece == "attn_out":
                    half, = at
                    ring_full.wait_ge(dve, job, ring_no(job, use) + 1)
                    dve.tensor_tensor(mid[:, 2 * half:2 * half + 2, :],
                                      ring_bank(job, use)[:, 0:S].rearrange("p (t d) -> p t d", t=2),
                                      xn[:, 2 * half:2 * half + 2, :], ALU.add).then_inc(bank_free(job, use).handle, 1)
                elif piece == "hidden_stats":
                    bank_free(job, ("attn_out", 0)).wait_ge(dve, job, times_used(job, ("attn_out", 0)) + 1)
                    bank_free(job, ("attn_out", 1)).wait_ge(dve, job, times_used(job, ("attn_out", 1)) + 1)
                    norm_statistics(job, "hidden", lambda tt: mid[:, tt, :])
                elif piece == "hidden_norm":
                    normalise(job, "hidden", lambda tt: mid[:, tt, :], lambda tt: mid[:, tt, :]
                              ).then_inc(mid_ready.handle, 1)
                elif piece == "split_hidden":
                    act_used.wait_ge(dve, job.before, 0)
                    bank_free(job, ("hidden",)).wait_ge(dve, job, times_used(job, ("hidden",)) + 1)
                    dve.tensor_copy(h_hi[:, job.parity, :], acc[:, job.parity, :]).then_inc(h_hi_ready.handle, 1)
                    h_hi_ready.wait_ge(dve, job, 1)
                    dve.tensor_tensor(h_lo[:, job.parity, :], acc[:, job.parity, :],
                                      h_hi[:, job.parity, :].bitcast(F32), ALU.subtract
                                      ).then_inc(h_ready.handle, 1)
                elif piece == "route":
                    ring_full.wait_ge(dve, job, ring_no(job, use) + 1)
                    dve.tensor_copy(logits[:, :, :], ring_bank(job, use)[:, 0:TT * E].rearrange(
                        "p (t e) -> p t e", t=TT)).then_inc(bank_free(job, use).handle, 1)
                    bank_free(job, use).wait_ge(dve, job, times_used(job, use) + 1, apart=True)
                    for tt in range(TT):
                        ins = dve.max(top8[:, tt, :], logits[:, tt, :])
                    ins.then_inc(top_ready.handle, 1)
                    top_ready.wait_ge(dve, job, 1)
                    dve.tensor_tensor(gap[:, :], top8[:, :, 1], top8[:, :, 0], ALU.subtract
                                      ).then_inc(gap_ready.handle, 1)
                    for tt in range(TT):
                        ins = dve.max_index(top8_at[:, tt, :], top8[:, tt, :], logits[:, tt, :])
                    ins.then_inc(top_at_ready.handle, 1)
                elif piece == "gate":
                    top_at_ready.wait_ge(dve, job, 1)
                    dve.tensor_copy(top_at[:, :, :], top8_at[:, :, 0:2].rearrange("p t n -> p n t")
                                    ).then_inc(chosen_ready.handle, 1)
                    chosen_ready.wait_ge(dve, job, 1)
                    dve.tensor_tensor(chosen[:, :, :],
                                      expert_no[:, :].unsqueeze(1).broadcast_to([P, 2 * TT, E]),
                                      top_at[:, :, :].rearrange("p n t -> p (n t)").unsqueeze(2).broadcast_to(
                                          [P, 2 * TT, E]), ALU.is_equal)
                    gap_exp_ready.wait_ge(dve, job, 1)
                    dve.tensor_scalar(gate_den[:, :], gap_exp[:, :], 1.0, None, ALU.add).then_inc(gate_step.handle, 1)
                    gate_step.wait_ge(dve, job, 1)
                    dve.reciprocal(gates[:, 0, :], gate_den[:, :]).then_inc(gate_step.handle, 1)
                    gate_step.wait_ge(dve, job, 2)
                    dve.tensor_tensor(gates[:, 1, :], gates[:, 0, :], gap_exp[:, :], ALU.mult
                                      ).then_inc(gate_step.handle, 1)
                    gate_step.wait_ge(dve, job, 3)
                    dve.tensor_tensor(chosen[:, :, :], chosen[:, :, :], gates[:, :, :].rearrange(
                        "p n t -> p (n t)").unsqueeze(2).broadcast_to([P, 2 * TT, E]), ALU.mult
                                      ).then_inc(gate_step.handle, 1)
                    gate_step.wait_ge(dve, job, 4)
                    dve.tensor_tensor(gate_w[:, :, :], chosen[:, 0:TT, :], chosen[:, TT:2 * TT, :], ALU.add
                                      ).then_inc(gate_step.handle, 1)
                    gate_step.wait_ge(dve, job, 5)
                    dve.tensor_copy(gate_hi[:, :, :], gate_w[:, :, :]).then_inc(gate_step.handle, 1)
                    gate_step.wait_ge(dve, job, 6)
                    dve.tensor_copy(gate_parts[:, :, 0:E], gate_hi[:, :, :].bitcast(F32))
                    dve.tensor_tensor(gate_parts[:, :, E:2 * E], gate_w[:, :, :], gate_hi[:, :, :].bitcast(F32),
                                      ALU.subtract).then_inc(gate_ready.handle, 1)

            def long(job, host, piece, *at):
                use = (piece,) + at
                if piece == "long_stats":
                    x_second_in.wait_ge(dve, job, 16)
                    for tt in range(TT):
                        ins = dve.bn_stats(long_stats[:, tt, :], x_second[:, tt, :])
                    ins.then_inc(long_stats_in.handle, 1)
                    long_stats_in.wait_ge(dve, job, 1, apart=True)
                    for tt in range(TT):
                        ins = dve.bn_aggr(long_moments[:, tt, :], long_stats[:, tt, :])
                    ins.then_inc(long_moments_in.handle, 1)
                    long_moments_in.wait_ge(dve, job, 1)
                    dve.tensor_scalar(long_var[:, :], long_moments[:, :, 1], EPS, None, ALU.add
                                      ).then_inc(long_var_in.handle, 1)
                elif piece == "long_norm":
                    long_rstd_in.wait_ge(dve, job, 1)
                    for tt in range(TT):
                        ins = dve.tensor_scalar(long_xn[:, tt, 0:D], x_second[:, tt, :], long_moments[:, tt, 0:1],
                                                long_rstd[:, tt:tt + 1], ALU.subtract, ALU.mult)
                    ins.then_inc(long_xn_ready.handle, 1)
                elif piece == "long_values":
                    b, = at
                    ring_full.wait_ge(dve, host, ring_no(host, use) + 1)
                    pair = ring_bank(host, use).rearrange("p (q n) -> p q n", q=2)
                    dve.reciprocal(long_rec[:, 2 * b:2 * b + 2], pair[:, :, D]).then_inc(long_recip.handle, 1)
                    long_recip.wait_ge(dve, job, b + 1)
                    for qt in range(2):
                        tt = 2 * b + qt
                        ins = dve.scalar_tensor_tensor(out=x_second[:, tt, :], in0=pair[:, qt, 0:D],
                                                       scalar=long_rec[:, tt:tt + 1], in1=x_second[:, tt, :],
                                                       op0=ALU.mult, op1=ALU.add)
                    ins.then_inc(bank_free(host, use).handle, 1)

            def expert_sums(job, t):
                if t >= LAG and (t - LAG) % FC == FC - 1:
                    e = (t - LAG) // FC
                    hidden_free.wait_ge(dve, job, gates_use(e) + 1)
                    act_used.wait_ge(dve, job, FC * (e + 1))
                    added.wait_ge(dve, job, max(e - 1, 0))
                    dve.tensor_tensor(gated[:, e % 2, :], ps_y[:, :], gate_bc[:, e % 2, :], ALU.mult
                                      ).then_inc(y_free.handle, 1)

            def middle_tick(job, t):
                if t < HID:
                    hidden_free.wait_ge(dve, job, hidden_use(t) + 1)
                    act_used.wait_ge(dve, job, t - 3)
                    if t in HIGH_BY_SCALAR:
                        scalar_hi_ready.wait_ge(dve, job, HIGH_BY_SCALAR.index(t) + 1)
                    else:
                        dve.tensor_copy(act_hi[:, t % 4, :], act[:, t % 2, :]).then_inc(act_hi_ready.handle, 1)
                        act_hi_ready.wait_ge(dve, job, t + 1 - sum(n < t for n in HIGH_BY_SCALAR))
                    dve.tensor_tensor(act_lo[:, t % 4, :], act[:, t % 2, :], act_hi[:, t % 4, :].bitcast(F32),
                                      ALU.subtract).then_inc(act_ready.handle, 1)
                if t == 3:
                    bias_full.wait_ge(dve, job, 1)
                    dve.tensor_tensor(acc[:, job.parity, :], ps_attn[:, :], acc[:, job.parity, :], ALU.add
                                      ).then_inc(bias_used.handle, 1)

            def end_tick(job, t):
                if t == 3:
                    y_free.wait_ge(dve, job, E + 1)
                    for tt in range(TT):
                        ins = dve.bn_stats(end_stats[:, tt, :], end_rows[:, tt, :])
                    ins.then_inc(end_stats_in.handle, 1)
                    end_stats_in.wait_ge(dve, job, 1, apart=True)
                    for tt in range(TT):
                        ins = dve.bn_aggr(end_moments[:, tt, :], end_stats[:, tt, :])
                    ins.then_inc(end_moments_in.handle, 1)
                    end_moments_in.wait_ge(dve, job, 1)
                    dve.tensor_scalar(end_var[:, :], end_moments[:, :, 1], EPS, None, ALU.add
                                      ).then_inc(end_var_in.handle, 1)
                if t == 5:
                    end_rstd_in.wait_ge(dve, job, 1)
                    for tt in range(TT):
                        ins = dve.tensor_scalar(end_rows[:, tt, :], end_rows[:, tt, :], end_moments[:, tt, 0:1],
                                                end_rstd[:, tt:tt + 1], ALU.subtract, ALU.mult)
                    ins.then_inc(end_normed.handle, 1)
                if t == 7:
                    end_scaled.wait_ge(dve, job, 1)
                    dve.tensor_tensor(end_rows[:, :, :], end_rows[:, :, :], x_plus[:, job.parity, :, :], ALU.add
                                      ).then_inc(result_ready.handle, 1)

            def split_expert(e):
                dve.wait_ge(weights_hi, e + 1)
                dve.tensor_tensor(w1_lo[:, e, :], stage[e % 2][:, 0:F], w1_hi[:, e, :].bitcast(F32), ALU.subtract)
                dve.tensor_tensor(w2_lo[:, e, :, :].rearrange("p c n -> p (c n)"), stage[e % 2][:, F:2 * F],
                                  w2_hi[:, e, :, :].rearrange("p c n -> p (c n)").bitcast(F32), ALU.subtract
                                  ).then_inc(weights_lo, 1)

            dve.memset(values[:, :, :, :], 0.0).then_inc(const_dve, 1)
            dve.memset(shift_cols[:, :, :, :, :], 0.0)
            dve.memset(long_xn[:, :, D:D + 1], float(RATE))
            dve.memset(power[:, :], -0.5)
            dve.memset(ones_row[:, :], 1.0)
            for e in range(E):
                dve.memset(expert_no[:, e:e + 1], float(e))
            dve.wait_ge(const_dve, 1)
            dve.memset(values[:, :, :, HD:HD + 1], 1.0)
            dve.wait_ge(const_pool, 2)
            dve.tensor_copy(ident_bf[:, :], ident[:, :])
            dve.tensor_reduce(phase_of[:, :], ident[:, :].rearrange("p (m r) -> p r m", r=RATE), AX.X, ALU.add)
            dve.tensor_reduce(head_rows[:, :], ident[:, :].rearrange("p (a i d) -> p i a d", a=4, i=4), AX.XY,
                              ALU.add)
            dve.tensor_reduce(shift_rows[:, :], ident[:, :].rearrange("p (a d) -> p a d", d=8)[:, :, 0:2], AX.XY,
                              ALU.add)
            dve.tensor_tensor(expert_rows[:, :], ident[0:2 * E, 0:E], ident[0:2 * E, E:2 * E], ALU.add
                              ).then_inc(const_dve, 1)
            dve.wait_ge(const_dve, 2)
            dve.tensor_scalar(head_shift[:, :], head_rows[:, :], shift_rows[:, 0:1], None, ALU.mult
                              ).then_inc(const_dve, 1)
            dve.wait_ge(const_dve, 3)
            for j in range(GROUPS):
                ins = dve.tensor_copy(k_diag[96:P, j, :, :],
                                      head_shift[96:P, :].unsqueeze(2).broadcast_to([32, 4, TOK]))
            ins.then_inc(const_dve, 1)
            dve.wait_ge(set_done, 1)

            def step(jobs, s):
                on_ticks(front, long, middle_tick, end_tick, jobs, s,
                         split_expert if s == -1 else None, sums=expert_sums)

            run_steps(dve, step)

        @block.gpsimd
        def _(pool):
            def front(job, piece, *at):
                rows_in = x_first if job.kind == "A" else x_second
                if piece in ("stats", "hidden_stats"):
                    n = norm_no("norm" if piece == "stats" else "hidden")
                    norm_var[n].wait_ge(pool, job, 1)
                    pool.tensor_tensor(rstd[:, n, :], var_eps[:, n, :], power[:, :], ALU.pow
                                       ).then_inc(norm_rstd[n].handle, 1)
                elif piece == "residual":
                    xn_ready.wait_ge(pool, job, 1)
                    result_ready.wait_ge(pool, job.before, 0)
                    pool.tensor_tensor(x_plus[:, job.parity, :, :], rows_in[:, :, :],
                                      b2_half[:, :].unsqueeze(1).broadcast_to([P, TT, D]), ALU.add
                                      ).then_inc(rows_used.handle, 1)
                elif piece == "mask":
                    b, = at
                    if b == 0:
                        values_done.wait_ge(pool, job, 0)
                        keys_in.wait_ge(pool, job, 16 * 3, apart=True)
                    cols = slice(b * S, (b + 1) * S)
                    for i in range(2):
                        ins = pool.tensor_scalar(k_diag[0:96, :, i, cols], k4_groups[0:96, :, cols],
                                                 head_rows[0:96, i:i + 1], 0.0, ALU.mult, ALU.add)
                    ins.then_inc(k_diag_first.handle, 1)
                elif piece == "head":
                    k, = at
                    bank_free(job, ("head", k)).wait_ge(pool, job, times_used(job, ("head", k)) + 1, apart=True)
                    both = probs[:, k % 4, 0:2 * P].rearrange("p (a q) -> p a q", a=2)
                    pool.affine_select(out=both, in_=both, compare_op=ALU.is_ge, fill=0.0, base=0,
                                       pattern=[[0, 2], [1, P]], channel_multiplier=-1
                                       ).then_inc(probs_ready.handle, 1)

            def long(job, host, piece, *at):
                if piece == "long_stats":
                    long_var_in.wait_ge(pool, job, 1)
                    pool.tensor_tensor(long_rstd[:, :], long_var[:, :], power[:, :], ALU.pow
                                       ).then_inc(long_rstd_in.handle, 1)
                elif piece == "long_scores":
                    b, = at
                    bank_free(host, ("long_scores", b)).wait_ge(pool, host, times_used(host, ("long_scores", b)) + 1)
                    pairs = long_e[:, b, :, :].rearrange("p k (n r) -> p (k n) r", r=RATE)
                    pool.tensor_tensor(pairs, pairs,
                                       phase_of[:, :].unsqueeze(1).broadcast_to([P, 2 * S // RATE, RATE]), ALU.mult
                                       ).then_inc(long_masked.handle, 1)

            def middle_tick(job, t):
                if t >= LAG and (t - LAG) % FC == FC - 1:
                    e = (t - LAG) // FC
                    y_free.wait_ge(pool, job, e + 1)
                    if e == 0:
                        bias_used.wait_ge(pool, job, 1)
                    added.wait_ge(pool, job, e)
                    pool.tensor_tensor(acc[:, job.parity, :], acc[:, job.parity, :], gated[:, e % 2, :], ALU.add
                                       ).then_inc(added.handle, 1)

            def end_tick(job, t):
                if t == 3:
                    end_var_in.wait_ge(pool, job, 1)
                    pool.tensor_tensor(end_rstd[:, :], end_var[:, :], power[:, :], ALU.pow
                                       ).then_inc(end_rstd_in.handle, 1)
                if t == 5:
                    end_normed.wait_ge(pool, job, 1)
                    pool.tensor_tensor(end_rows[:, :, :], end_rows[:, :, :],
                                       g2_half[:, :].unsqueeze(1).broadcast_to([P, TT, D]), ALU.mult
                                       ).then_inc(end_scaled.handle, 1)

            pool.memset(ident[:, :], 0.0)
            pool.memset(causal[:, :], 0.0).then_inc(const_pool, 1)
            pool.wait_ge(const_pool, 1)
            pool.affine_select(out=ident[:, :], in_=ident[:, :], compare_op=ALU.not_equal, fill=1.0, base=0,
                               pattern=[[-1, P]], channel_multiplier=1).then_inc(const_pool, 1)
            pool.affine_select(out=causal[:, :], in_=causal[:, :], compare_op=ALU.is_ge, fill=MASKED, base=0,
                               pattern=[[-1, P]], channel_multiplier=1).then_inc(const_pool, 1)
            pool.wait_ge(const_dve, CONSTANTS)

            def step(jobs, s):
                on_ticks(front, long, middle_tick, end_tick, jobs, s)

            run_steps(pool, step)


_INS = ['L0_attn_x', 'L0_ffn_w_qkv', 'L0_ffn_w_o', 'L0_ffn_g1', 'L0_ffn_b1', 'L0_ffn_wg', 'L0_ffn_w1',
        'L0_ffn_bb1', 'L0_ffn_w2', 'L0_ffn_bb2', 'L0_ffn_g2', 'L0_ffn_b2']


def kernel(**inputs):
    import numpy as _np
    import concourse.bacc as _bacc
    from concourse import mybir as _mybir
    from concourse.bass_utils import run_bass_kernel_spmd as _run

    nc = _bacc.Bacc("TRN2", target_bir_lowering=False, num_devices=1)
    arrays, args = {}, []
    for name in _INS:
        a = _np.ascontiguousarray(inputs[name])
        arrays[f"in_{name}"] = a
        args.append(nc.dram_tensor(f"in_{name}", a.shape, _mybir.dt.from_np(a.dtype), kind="ExternalInput").ap())
    out = nc.dram_tensor("out_rows", [SEQS, S, D], _mybir.dt.float32, kind="ExternalOutput").ap()
    build(nc, *args, out)
    r = _run(nc, [arrays], core_ids=[0])
    return r.results[0]["out_rows"]
```
